# Optimizing a Trainium2 kernel written in Bass

```python
import numpy as np
import jax
import jax.numpy as jnp

def _softmax(x, axis=-1):
    return jax.nn.softmax(x, axis=axis)
def _gelu(x):
    return jax.nn.gelu(x, approximate=True)
def _silu(x):
    return jax.nn.silu(x)
def _sigmoid(x):
    return jax.nn.sigmoid(x)
def _layernorm(x, axis=-1, eps=1e-5):
    m = jnp.mean(x, axis=axis, keepdims=True)
    v = jnp.var(x, axis=axis, keepdims=True)
    return (x - m) / jnp.sqrt(v + eps)
def _scatter_add(tgt, idx, src, axis=0):
    return tgt.at[idx].add(src)
def _segment_sum(src, seg, n):
    return jax.ops.segment_sum(src, seg, n)

kernel_name = 'mk_conv_seq_d1_conv_nchw128_3d322e'

def setup_inputs(seed: int = 0):
    np.random.seed(seed)
    _w = jnp.asarray
    def _rec_inputs():
        import jax
        import jax.numpy as jnp
        _gk = jax.random.key(seed)
        x = -0.0003957 + 1 * jax.random.normal(jax.random.fold_in(_gk, 1), (32, 128, 56, 56), jnp.float32)
        return x
    x = _rec_inputs()
    def _L0_conv_setup():
        import jax, jax.numpy as jnp
        import numpy as np
        NBITS = 3
        BN_EPS = 1e-05

        def lsq_quantize(w, alpha):
            Qn = -2 ** (NBITS - 1)
            Qp = 2 ** (NBITS - 1) - 1
            g = 1.0 / jnp.sqrt(float(w.size) * Qp)
            alpha_s = alpha * g + jax.lax.stop_gradient(alpha - alpha * g)
            wc = jnp.clip(w / alpha_s, Qn, Qp)
            wq = wc + jax.lax.stop_gradient(jnp.round(wc) - wc)
            return wq * alpha_s

        def conv3x3_decomposed(x, wq):
            B, C, H, W = x.shape
            xp = jnp.pad(x, ((0, 0), (0, 0), (1, 1), (1, 1)))
            out = jnp.zeros((B, wq.shape[0], H, W), dtype=x.dtype)
            for kh in range(3):
                for kw in range(3):
                    out = out + jnp.einsum('bchw,oc->bohw', xp[:, :, kh:kh + H, kw:kw + W], wq[:, :, kh, kw])
            return out

        def batchnorm(x, gamma, beta):
            mean = jnp.mean(x, axis=(0, 2, 3), keepdims=True)
            var = jnp.var(x, axis=(0, 2, 3), keepdims=True)
            xhat = (x - mean) * jax.lax.rsqrt(var + BN_EPS)
            return gamma[None, :, None, None] * xhat + beta[None, :, None, None]
        key = jax.random.key(seed)
        ks = jax.random.split(key, 4)
        B, C, H, W = (32, 128, 56, 56)
        x = jax.random.normal(ks[0], (B, C, H, W), dtype=jnp.float32)
        w1 = jax.random.normal(ks[1], (C, C, 3, 3), dtype=jnp.float32) * 0.05
        w2 = jax.random.normal(ks[2], (C, C, 3, 3), dtype=jnp.float32) * 0.05
        alpha1 = jnp.array([0.02], dtype=jnp.float32)
        alpha2 = jnp.array([0.02], dtype=jnp.float32)
        gamma1 = jnp.ones((C,), dtype=jnp.float32)
        beta1 = jnp.zeros((C,), dtype=jnp.float32)
        gamma2 = jnp.ones((C,), dtype=jnp.float32)
        beta2 = jnp.zeros((C,), dtype=jnp.float32)
        return {'x': x, 'w1': w1, 'alpha1': alpha1, 'gamma1': gamma1, 'beta1': beta1, 'w2': w2, 'alpha2': alpha2, 'gamma2': gamma2, 'beta2': beta2}
    _L0_conv_all = _L0_conv_setup()
    _L0_conv_in = {k: v for k, v in _L0_conv_all.items() if k in ('w1', 'alpha1', 'gamma1', 'beta1', 'w2', 'alpha2', 'gamma2', 'beta2', )}
    del _L0_conv_all

    return {
        "x": x,
        "L0_conv_w1": _L0_conv_in["w1"],
        "L0_conv_alpha1": _L0_conv_in["alpha1"],
        "L0_conv_gamma1": _L0_conv_in["gamma1"],
        "L0_conv_beta1": _L0_conv_in["beta1"],
        "L0_conv_w2": _L0_conv_in["w2"],
        "L0_conv_alpha2": _L0_conv_in["alpha2"],
        "L0_conv_gamma2": _L0_conv_in["gamma2"],
        "L0_conv_beta2": _L0_conv_in["beta2"],
    }

def reference(x, L0_conv_w1, L0_conv_alpha1, L0_conv_gamma1, L0_conv_beta1, L0_conv_w2, L0_conv_alpha2, L0_conv_gamma2, L0_conv_beta2):
    import jax
    import jax.numpy as jnp
    def _L0_conv_ref(x, w1, alpha1, gamma1, beta1, w2, alpha2, gamma2, beta2):
        import jax, jax.numpy as jnp
        import numpy as np
        NBITS = 3
        BN_EPS = 1e-05

        def lsq_quantize(w, alpha):
            Qn = -2 ** (NBITS - 1)
            Qp = 2 ** (NBITS - 1) - 1
            g = 1.0 / jnp.sqrt(float(w.size) * Qp)
            alpha_s = alpha * g + jax.lax.stop_gradient(alpha - alpha * g)
            wc = jnp.clip(w / alpha_s, Qn, Qp)
            wq = wc + jax.lax.stop_gradient(jnp.round(wc) - wc)
            return wq * alpha_s

        def conv3x3_decomposed(x, wq):
            B, C, H, W = x.shape
            xp = jnp.pad(x, ((0, 0), (0, 0), (1, 1), (1, 1)))
            out = jnp.zeros((B, wq.shape[0], H, W), dtype=x.dtype)
            for kh in range(3):
                for kw in range(3):
                    out = out + jnp.einsum('bchw,oc->bohw', xp[:, :, kh:kh + H, kw:kw + W], wq[:, :, kh, kw])
            return out

        def batchnorm(x, gamma, beta):
            mean = jnp.mean(x, axis=(0, 2, 3), keepdims=True)
            var = jnp.var(x, axis=(0, 2, 3), keepdims=True)
            xhat = (x - mean) * jax.lax.rsqrt(var + BN_EPS)
            return gamma[None, :, None, None] * xhat + beta[None, :, None, None]
        residual = x
        out = conv3x3_decomposed(x, lsq_quantize(w1, alpha1))
        out = jax.nn.relu(batchnorm(out, gamma1, beta1))
        out = conv3x3_decomposed(out, lsq_quantize(w2, alpha2))
        out = batchnorm(out, gamma2, beta2)
        out = jax.nn.relu(out + residual)
        return out

    def _gn(v, G=32, eps=1e-5):
        B_, C_, H_, W_ = v.shape
        g = v.reshape(B_, G, C_ // G, H_, W_)
        m = jnp.mean(g, axis=(2, 3, 4), keepdims=True)
        s = jnp.var(g, axis=(2, 3, 4), keepdims=True)
        return ((g - m) / jnp.sqrt(s + eps)).reshape(v.shape)

    def _ln_c(v, eps=1e-6):
        m = jnp.mean(v, axis=1, keepdims=True)
        s = jnp.var(v, axis=1, keepdims=True)
        return (v - m) / jnp.sqrt(s + eps)

    def _ln_t(v, eps=1e-5):
        m = jnp.mean(v, axis=-1, keepdims=True)
        s = jnp.var(v, axis=-1, keepdims=True)
        return (v - m) / jnp.sqrt(s + eps)

    def _to_tokens(v):
        B_, C_, H_, W_ = v.shape
        return v.reshape(B_, C_, H_ * W_).transpose(0, 2, 1)
    def _from_tokens(t, like):
        B_, C_, H_, W_ = like.shape
        return t.transpose(0, 2, 1).reshape(B_, C_, H_, W_)

    x = _L0_conv_ref(x, L0_conv_w1, L0_conv_alpha1, L0_conv_gamma1, L0_conv_beta1, L0_conv_w2, L0_conv_alpha2, L0_conv_gamma2, L0_conv_beta2)
    return x


_drawn_inputs = setup_inputs


def setup_inputs(seed=0):
    import zlib

    import numpy as np

    out = dict(_drawn_inputs(seed))
    spreads = {'L0_conv_gamma1': (1.0, 0.2),
     'L0_conv_beta1': (0.0, 0.1),
     'L0_conv_gamma2': (1.0, 0.2),
     'L0_conv_beta2': (0.0, 0.1)}
    factors = {}
    for name, (base, spread) in spreads.items():
        noise = np.random.default_rng([zlib.crc32(name.encode()), seed]).standard_normal(out[name].shape)
        drawn = base * np.exp(spread * noise) if base else spread * noise
        out[name] = jnp.asarray(drawn.astype(out[name].dtype))
    for name, factor in factors.items():
        out[name] = (out[name] * factor).astype(out[name].dtype)
    return out
```

```python
from contextlib import ExitStack

import concourse.bass as bass
import numpy as np
from concourse import mybir

F32 = mybir.dt.float32
F32R = mybir.dt.float32r
BF16 = mybir.dt.bfloat16
ALU = mybir.AluOpType
ACT = mybir.ActivationFunctionType

BN_EPS = 1e-5
Q_MIN, Q_MAX = -4.0, 3.0
ROUND = 12582912.0

SLOTS = 12
XBUFS = 4


def residual_block(nc, x, w1, alpha1, gamma1, beta1, w2, alpha2, gamma2, beta2, out):
    IMAGES, C, H, W = x.shape
    TAPS = w1.shape[2] * w1.shape[3]
    PIX = H * W
    ROWS = 8
    CHUNKS = H // ROWS
    N = ROWS * W
    PITCH = W + 2
    LEAD = 2
    PLANE = LEAD + H * PITCH
    PLANE_SIZE = (PLANE + 7) // 8 * 8
    PARTS = [(0, 9), (9, 33), (33, 56)]
    NP = len(PARTS)
    CHUNK_NEEDS = [next(k + 1 for k, (_, end) in enumerate(PARTS) if end >= min(H, ROWS * (j + 1) + 1))
                   for j in range(CHUNKS)]
    SPILL = IMAGES - SLOTS
    STEPS = 2 * IMAGES
    PADS = 10
    LSQ_G = float(np.float32(1.0) / np.sqrt(np.float32(float(C * C * TAPS) * Q_MAX)))
    assert C == 128 and H % ROWS == 0 and IMAGES % 4 == 0 and SLOTS % 2 == 0 and SPILL % 2 == 0

    xi = x.rearrange("b c h w -> b c (h w)")
    oi = out.rearrange("b c h w -> b c (h w)")
    y1_dram = nc.dram_tensor("conv1_spill", (SPILL, C, PIX), F32, kind="Internal").ap()
    y2_dram = nc.dram_tensor("conv2_spill", (SPILL, C, PIX), F32, kind="Internal").ap()

    with ExitStack() as ctx:
        def sb(name, shape, dt):
            return ctx.enter_context(nc.sbuf_tensor(name, shape, dt))

        def sem(name):
            return ctx.enter_context(nc.semaphore(name))

        slots = sb("slots", [C, SLOTS, PIX], F32)
        wT = [sb(f"w{k + 1}T", [C, TAPS, C], F32R) for k in range(2)]
        base = (nc.sbuf_base + 31) // 32 * 32
        arena = sb("plane_arena", [C, 4 * PLANE_SIZE], F32)
        hi = [nc.alloc_sbuf_tensor_at(f"hi{b}", [C, PLANE], F32R, offset=base + (2 * b) * PLANE_SIZE * 4)
              for b in range(2)]
        lo = [nc.alloc_sbuf_tensor_at(f"lo{b}", [C, PLANE], F32R, offset=base + (2 * b + 1) * PLANE_SIZE * 4)
              for b in range(2)]
        xbuf = [nc.alloc_sbuf_tensor_at(f"xbuf{b}", [C, PIX], F32, offset=base + b * PLANE_SIZE * 4)
                for b in range(XBUFS)]
        ident = sb("ident", [C, C], BF16)
        alpha_in = sb("alpha_in", [C, 2], F32)
        gb = sb("gamma_beta", [C, 4], F32)
        alpha = sb("alpha_s", [C, 2], F32)
        tiny = sb("tiny", [C, 16], F32)
        minus_half = sb("minus_half", [C, 1], F32)
        affine = sb("affine", [C, 2, 2], F32)
        chunk_stats = sb("chunk_stats", [C, CHUNKS, 6], F32)
        image_mv = sb("image_mv", [C, 2], F32)
        image_stats = sb("image_stats", [C, 2, IMAGES, 3], F32)
        total_mv = sb("total_mv", [C, 2], F32)
        psum = ctx.enter_context(nc.psum_tensor("conv_psum", [C, CHUNKS, 512], F32))
        psum_t = ctx.enter_context(nc.psum_tensor("transpose_psum", [C, 1024], BF16))

        w_raw = [slots[:, SLOTS - 1, k * C * TAPS:(k + 1) * C * TAPS] for k in range(2)]
        w_int = [slots[:, SLOTS - 2, k * C * TAPS:k * C * TAPS + C * TAPS // 2].bitcast(BF16) for k in range(2)]

        w_landed = [sem("w1_landed"), sem("w2_landed")]
        small_landed = sem("small_landed")
        ident_zeroed = sem("ident_zeroed")
        ident_ready = sem("ident_ready")
        half_ready = sem("half_ready")
        pads_ready = sem("pads_ready")
        dve_step = sem("dve_step")
        w_int_ready = sem("w_int_ready")
        transposed = sem("transposed")
        wT_ready = sem("wT_ready")
        x_landed = [sem(f"x_landed{b}") for b in range(2)]
        y1_landed = [sem(f"y1_landed{b}") for b in range(2)]
        y1_stored = [sem(f"y1_stored{b}") for b in range(2)]
        y2_stored = [sem(f"y2_stored{b}") for b in range(2)]
        hi_ready = sem("hi_ready")
        relu_ready = sem("relu_ready")
        lo_ready = sem("lo_ready")
        chunk_done = sem("chunk_done")
        evac_done = sem("evac_done")
        bn_done = sem("bn_done")
        aggregated = sem("aggregated")
        image_done = sem("image_done")
        powed = sem("powed")
        var_ready = sem("var_ready")
        affine_ready = sem("affine_ready")
        res_landed = [sem(f"res_landed{b}") for b in range(XBUFS)]
        y2_landed = [sem(f"y2_landed{b}") for b in range(XBUFS)]
        added = sem("added")
        final_ready = sem("final_ready")
        out_stored = [sem(f"out_stored{b}") for b in range(XBUFS)]

        def slot(p, a=0, b=PIX):
            if isinstance(p, int):
                return slots[:, p % SLOTS, a:b]
            return slots[:, bass.ds(p % SLOTS, 1), a:b].rearrange("c s n -> c (s n)")

        def dram_image(t, i):
            if isinstance(i, int):
                return t[i]
            return t[bass.ds(i, 1)].rearrange("b c n -> c (b n)")

        def rows_of(ap, rows):
            return ap.rearrange("c (r w) -> c r w", r=rows)

        def window(plane, r0, r1, shift):
            if shift < 0:
                v = plane[:, LEAD - 2:LEAD - 2 + H * PITCH].rearrange("c (r w) -> c r w", r=H)
                return v[:, r0:r1, 2 + shift:2 + shift + W]
            v = plane[:, LEAD:LEAD + H * PITCH].rearrange("c (r w) -> c r w", r=H)
            return v[:, r0:r1, shift:shift + W]

        block = ctx.enter_context(nc.Block())

        @block.sync
        def _(sp):
            def load_x(g, b):
                sp.dma_start(slot(g), dram_image(xi, g)).then_inc(x_landed[b], 16)

            def split_over(g):
                sp.wait_ge(lo_ready, NP * g + NP)

            def step_over(g):
                sp.wait_ge(bn_done, CHUNKS * g + CHUNKS)

            sp.dma_start(w_raw[0], w1.rearrange("o c a b -> o (c a b)")).then_inc(w_landed[0], 16)
            load_x(0, 0)
            sp.dma_start(w_raw[1], w2.rearrange("o c a b -> o (c a b)")).then_inc(w_landed[1], 16)
            load_x(1, 1)

            def phase1_load(k, b, reuse):
                split_over(k)
                if reuse:
                    old = k + 2 - SLOTS
                    step_over(old)
                    sp.wait_ge(y1_stored[b], half(old) * 16 + 16)
                load_x(k + 2, b)

            def half(v):
                return v // 2

            def phase1_store(k, b, first=False):
                step_over(k)
                if not first:
                    sp.wait_ge(y1_stored[b], half(k) * 16)
                sp.dma_start(dram_image(y1_dram, k), slot(k)).then_inc(y1_stored[b], 16)

            for b in range(2):
                phase1_load(b, b, False)
                phase1_store(b, b, first=True)
            with sp.Fori(1, (SLOTS - 2) // 2) as i:
                for b in range(2):
                    phase1_load(i * 2 + b, b, False)
                    phase1_store(i * 2 + b, b)
            with sp.Fori((SLOTS - 2) // 2, SPILL // 2) as i:
                for b in range(2):
                    phase1_load(i * 2 + b, b, True)
                    phase1_store(i * 2 + b, b)
            with sp.Fori(SPILL // 2, (IMAGES - 2) // 2) as i:
                for b in range(2):
                    phase1_load(i * 2 + b, b, True)
            for b in range(2):
                sp.wait_ge(y1_stored[b], 16 * (SPILL // 2))

            def phase2_load(m, b):
                split_over(IMAGES + m - 2)
                step_over(IMAGES + m - SLOTS)
                sp.wait_ge(y2_stored[b], half(m - SLOTS) * 16 + 16)
                sp.dma_start(slot(SPILL + m), dram_image(y1_dram, m - SLOTS)).then_inc(y1_landed[b], 16)

            def phase2_store(m, b, first=False):
                step_over(IMAGES + m)
                if not first:
                    sp.wait_ge(y2_stored[b], half(m) * 16)
                sp.dma_start(dram_image(y2_dram, m), slot(SPILL + m)).then_inc(y2_stored[b], 16)

            for b in range(2):
                phase2_store(b, b, first=True)
            with sp.Fori(1, (SLOTS - 2) // 2) as i:
                for b in range(2):
                    phase2_store(i * 2 + b, b)
            with sp.Fori((SLOTS - 2) // 2, SPILL // 2) as i:
                for b in range(2):
                    phase2_load(i * 2 + b + 2, b)
                    phase2_store(i * 2 + b, b)
            with sp.Fori(SPILL // 2, (IMAGES - 2) // 2) as i:
                for b in range(2):
                    phase2_load(i * 2 + b + 2, b)
            for b in range(2):
                sp.wait_ge(y2_stored[b], 16 * (SPILL // 2))

            def load_residual(q, b):
                sp.dma_start(xbuf[b][:, :], dram_image(xi, (q + 2 * SPILL) % IMAGES)).then_inc(res_landed[b], 16)

            def load_y2(q, b):
                sp.wait_ge(out_stored[(q - SLOTS) % XBUFS if isinstance(q, int) else b],
                           (q - SLOTS) // XBUFS * 16 + 16)
                sp.dma_start(slot(q + 2 * SPILL), dram_image(y2_dram, q - SLOTS)).then_inc(y2_landed[b], 16)

            for b in range(XBUFS):
                sp.wait_ge(chunk_done, CHUNKS * (STEPS - 1 + b // 2))
                load_residual(b, b)
            with sp.Fori(1, SLOTS // XBUFS) as i:
                for b in range(XBUFS):
                    sp.wait_ge(added, i * XBUFS + (b - XBUFS + 1))
                    load_residual(i * XBUFS + b, b)
            with sp.Fori(SLOTS // XBUFS, IMAGES // XBUFS) as i:
                for b in range(XBUFS):
                    sp.wait_ge(added, i * XBUFS + (b - XBUFS + 1))
                    load_residual(i * XBUFS + b, b)
                    load_y2(i * XBUFS + b, b)
            for b in range(XBUFS):
                sp.wait_ge(out_stored[b], 16 * (IMAGES // XBUFS))

        @block.gpsimd
        def _(pool):
            nc.gpsimd.memset(minus_half[:, :], -0.5).then_inc(half_ready, 1)
            nc.gpsimd.memset(ident[:, :], 0.0).then_inc(ident_zeroed, 1)
            pool.wait_ge(ident_zeroed, 1)
            nc.gpsimd.affine_select(out=ident[:, :], in_=ident[:, :], compare_op=ALU.not_equal, fill=1.0, base=0,
                                    pattern=[[-1, C]], channel_multiplier=1).then_inc(ident_ready, 1)
            pool.wait_ge(half_ready, 1)
            for k in range(2):
                pool.wait_ge(var_ready, k + 1)
                nc.gpsimd.tensor_tensor(tiny[:, 1:2], tiny[:, 0:1], minus_half[:, :], ALU.pow).then_inc(powed, 1)

        @block.scalar
        def _(act):
            for k, a in enumerate((alpha1, alpha2)):
                act.dma_start(alpha_in[:, k:k + 1], a.rearrange("(a n) -> a n", a=1).to_broadcast([C, 1])
                              ).then_inc(small_landed, 16)
            for k, v in enumerate((gamma1, beta1, gamma2, beta2)):
                act.dma_start(gb[:, k:k + 1], v.rearrange("(c n) -> c n", n=1)).then_inc(small_landed, 16)

            for k in range(2):
                for first, n in ((0, 8), (8, 1)):
                    act.wait_ge(transposed, 2 * k + (1 if first == 0 else 2))
                    nc.scalar.copy(wT[k][:, first:first + n, :],
                                   psum_t[:, 0:n * C].rearrange("c (t o) -> c t o", t=n)).then_inc(wT_ready, 1)

            def split_x(g, b):
                act.wait_ge(x_landed[b], g // 2 * 16 + 16)
                if not (isinstance(g, int) and g < 2):
                    act.wait_ge(chunk_done, g * CHUNKS - CHUNKS)
                for r0, r1 in PARTS:
                    nc.scalar.copy(window(hi[b], r0, r1, 0),
                                   rows_of(slot(g, r0 * W, r1 * W), r1 - r0)).then_inc(hi_ready, 1)

            def split_y1(m, b, landed):
                if landed:
                    act.wait_ge(y1_landed[b], (m - SLOTS) // 2 * 16 + 16)
                act.wait_ge(chunk_done, m * CHUNKS + (IMAGES - 1) * CHUNKS)
                for r0, r1 in PARTS:
                    y = slot(m + SPILL, r0 * W, r1 * W)
                    nc.scalar.activation(window(hi[b], r0, r1, 0), rows_of(y, r1 - r0), ACT.Relu,
                                         bias=affine[:, 0, 1:2], scale=affine[:, 0, 0:1]).then_inc(hi_ready, 1)
                    nc.scalar.activation(y, y, ACT.Relu,
                                         bias=affine[:, 0, 1:2], scale=affine[:, 0, 0:1]).then_inc(relu_ready, 1)

            def evacuate(g, p):
                for j in range(CHUNKS):
                    act.wait_ge(chunk_done, g * CHUNKS + (j + 1))
                    nc.scalar.copy(slot(p + SLOTS, j * N, (j + 1) * N), psum[:, j, 0:N]).then_inc(evac_done, 1)

            split_x(0, 0)
            with act.Fori(0, (IMAGES - 2) // 2) as i:
                for b in range(2):
                    split_x(i * 2 + (b + 1), 1 - b)
                    evacuate(i * 2 + b, i * 2 + b)
            split_x(IMAGES - 1, 1)
            evacuate(IMAGES - 2, IMAGES - 2)
            evacuate(IMAGES - 1, IMAGES - 1)

            act.wait_ge(affine_ready, 1)
            split_y1(0, 0, False)
            with act.Fori(0, (SLOTS - 2) // 2) as i:
                for b in range(2):
                    split_y1(i * 2 + (b + 1), 1 - b, False)
                    evacuate(i * 2 + (b + IMAGES), i * 2 + (b + SPILL))
            split_y1(SLOTS - 1, 1, False)
            evacuate(IMAGES + SLOTS - 2, SPILL + SLOTS - 2)
            split_y1(SLOTS, 0, True)
            evacuate(IMAGES + SLOTS - 1, SPILL + SLOTS - 1)
            with act.Fori(SLOTS // 2, (IMAGES - 2) // 2) as i:
                for b in range(2):
                    split_y1(i * 2 + (b + 1), 1 - b, True)
                    evacuate(i * 2 + (b + IMAGES), i * 2 + (b + SPILL))
            split_y1(IMAGES - 1, 1, True)
            for m in (IMAGES - 2, IMAGES - 1):
                evacuate(IMAGES + m, SPILL + m)

            act.wait_ge(affine_ready, 2)

            def finish(q, b, first=False):
                act.wait_ge(added, q + 1)
                z = slot(q + 2 * SPILL)
                nc.scalar.activation(z, z, ACT.Relu, bias=affine[:, 1, 1:2]).then_inc(final_ready, 1)
                act.wait_ge(final_ready, q + 1)
                if not first:
                    act.wait_ge(out_stored[b], q // XBUFS * 16)
                act.dma_start(dram_image(oi, (q + 2 * SPILL) % IMAGES), z).then_inc(out_stored[b], 16)

            for b in range(XBUFS):
                finish(b, b, first=True)
            with act.Fori(1, IMAGES // XBUFS) as i:
                for b in range(XBUFS):
                    finish(i * XBUFS + b, b)

        @block.vector
        def _(dve):
            steps = [0]

            def link(ins):
                steps[0] += 1
                ins.then_inc(dve_step, 1)
                dve.wait_ge(dve_step, steps[0])

            for k, plane in enumerate((*hi, *lo)):
                nc.vector.memset(plane[:, 0:LEAD].bitcast(F32), 0.0).then_inc(pads_ready, 1)
                nc.vector.memset(plane[:, LEAD:].rearrange("c (r w) -> c r w", r=H)[:, :, W:PITCH].bitcast(F32),
                                 0.0).then_inc(pads_ready, 1)
            for k in range(2):
                nc.vector.memset(image_stats[:, k, :, 0], float(PIX)).then_inc(pads_ready, 1)

            dve.wait_ge(small_landed, 6 * 16)
            link(nc.vector.tensor_scalar(tiny[:, 4:6], alpha_in[:, :], LSQ_G, None, ALU.mult))
            link(nc.vector.tensor_tensor(tiny[:, 6:8], alpha_in[:, :], tiny[:, 4:6], ALU.subtract))
            link(nc.vector.tensor_tensor(alpha[:, :], tiny[:, 4:6], tiny[:, 6:8], ALU.add))
            link(nc.vector.reciprocal(tiny[:, 2:4], alpha[:, :]))
            for k in range(2):
                dve.wait_ge(w_landed[k], 16)
                link(nc.vector.tensor_scalar(w_raw[k], w_raw[k], tiny[:, 2 + k:3 + k], Q_MAX, ALU.mult, ALU.min))
                link(nc.vector.tensor_scalar(w_raw[k], w_raw[k], Q_MIN, ROUND, ALU.max, ALU.add))
                nc.vector.tensor_scalar(w_int[k].rearrange("o (t c) -> o c t", t=TAPS),
                                        w_raw[k].rearrange("o (c t) -> o c t", t=TAPS),
                                        ROUND, None, ALU.subtract).then_inc(w_int_ready, 1)

            def lo_half(g, p, b, after_relu=None):
                for k, (r0, r1) in enumerate(PARTS):
                    dve.wait_ge(hi_ready, g * NP + (k + 1))
                    if after_relu is not None:
                        dve.wait_ge(relu_ready, after_relu * NP + (k + 1))
                    nc.vector.tensor_tensor(window(lo[b], r0, r1, 0), rows_of(slot(p, r0 * W, r1 * W), r1 - r0),
                                            window(hi[b], r0, r1, 0).bitcast(F32),
                                            ALU.subtract).then_inc(lo_ready, 1)

            def statistics(g, p, phase, n):
                for j in range(CHUNKS):
                    dve.wait_ge(evac_done, g * CHUNKS + (j + 1))
                    nc.vector.bn_stats(chunk_stats[:, j, :], slot(p + SLOTS, j * N, (j + 1) * N)).then_inc(bn_done, 1)
                dve.wait_ge(pads_ready, PADS)
                dve.wait_ge(bn_done, g * CHUNKS + CHUNKS)
                nc.vector.bn_aggr(image_mv[:, :], chunk_stats[:, :, :]).then_inc(aggregated, 1)
                dve.wait_ge(aggregated, g + 1)
                at = n if isinstance(n, int) else bass.ds(n, 1)
                st = image_stats[:, phase, n:n + 1, :] if isinstance(n, int) else image_stats[:, phase, bass.ds(n, 1), :]
                nc.vector.tensor_copy(st[:, :, 1], image_mv[:, 0:1]).then_inc(image_done, 1)
                nc.vector.tensor_scalar(st[:, :, 2], image_mv[:, 1:2], float(PIX), None,
                                        ALU.mult).then_inc(image_done, 1)

            def batchnorm_affine(phase):
                dve.wait_ge(image_done, 2 * IMAGES * (phase + 1))
                link(nc.vector.bn_aggr(total_mv[:, :], image_stats[:, phase, :, :]))
                al, gm, be = alpha[:, phase:phase + 1], gb[:, 2 * phase:2 * phase + 1], gb[:, 2 * phase + 1:2 * phase + 2]
                link(nc.vector.tensor_scalar(tiny[:, 8:9], total_mv[:, 1:2], al, al, ALU.mult, ALU.mult))
                nc.vector.tensor_scalar(tiny[:, 0:1], tiny[:, 8:9], BN_EPS, None, ALU.add).then_inc(var_ready, 1)
                dve.wait_ge(powed, phase + 1)
                r, v = tiny[:, 1:2], tiny[:, 0:1]
                link(nc.vector.tensor_scalar(tiny[:, 9:10], r, r, v, ALU.mult, ALU.mult))
                link(nc.vector.tensor_scalar(tiny[:, 10:11], tiny[:, 9:10], -0.5, 1.5, ALU.mult, ALU.add))
                link(nc.vector.tensor_scalar(tiny[:, 11:12], tiny[:, 10:11], r, al, ALU.mult, ALU.mult))
                link(nc.vector.tensor_scalar(affine[:, phase, 0:1], tiny[:, 11:12], gm, None, ALU.mult))
                link(nc.vector.tensor_scalar(tiny[:, 12:13], affine[:, phase, 0:1], -1.0, None, ALU.mult))
                nc.vector.tensor_scalar(affine[:, phase, 1:2], total_mv[:, 0:1], tiny[:, 12:13], be,
                                        ALU.mult, ALU.add).then_inc(affine_ready, 1)

            lo_half(0, 0, 0)
            with dve.Fori(0, (IMAGES - 2) // 2) as i:
                for b in range(2):
                    lo_half(i * 2 + (b + 1), i * 2 + (b + 1), 1 - b)
                    statistics(i * 2 + b, i * 2 + b, 0, i * 2 + b)
            lo_half(IMAGES - 1, IMAGES - 1, 1)
            statistics(IMAGES - 2, IMAGES - 2, 0, IMAGES - 2)
            statistics(IMAGES - 1, IMAGES - 1, 0, IMAGES - 1)
            batchnorm_affine(0)

            lo_half(IMAGES, SPILL, 0, after_relu=0)
            with dve.Fori(0, (IMAGES - 2) // 2) as i:
                for b in range(2):
                    lo_half(i * 2 + (b + 1 + IMAGES), i * 2 + (b + 1 + SPILL), 1 - b, after_relu=i * 2 + (b + 1))
                    statistics(i * 2 + (b + IMAGES), i * 2 + (b + SPILL), 1, i * 2 + b)
            lo_half(STEPS - 1, SPILL + IMAGES - 1, 1, after_relu=IMAGES - 1)
            statistics(STEPS - 2, SPILL + IMAGES - 2, 1, IMAGES - 2)
            statistics(STEPS - 1, SPILL + IMAGES - 1, 1, IMAGES - 1)
            batchnorm_affine(1)
            dve.wait_ge(affine_ready, 2)

            def add_residual(q, b, landed):
                dve.wait_ge(res_landed[b], q // XBUFS * 16 + 16)
                if landed:
                    dve.wait_ge(y2_landed[b], (q - SLOTS) // XBUFS * 16 + 16)
                z = slot(q + 2 * SPILL)
                nc.vector.scalar_tensor_tensor(out=z, in0=z, scalar=affine[:, 1, 0:1], in1=xbuf[b][:, :],
                                               op0=ALU.mult, op1=ALU.add).then_inc(added, 1)

            with dve.Fori(0, SLOTS // XBUFS) as i:
                for b in range(XBUFS):
                    add_residual(i * XBUFS + b, b, False)
            with dve.Fori(SLOTS // XBUFS, IMAGES // XBUFS) as i:
                for b in range(XBUFS):
                    add_residual(i * XBUFS + b, b, True)

        @block.tensor
        def _(pe):
            pe.wait_ge(ident_ready, 1)
            for k in range(2):
                pe.wait_ge(w_int_ready, k + 1)
                for first, n in ((0, 8), (8, 1)):
                    if (k, first) != (0, 0):
                        pe.wait_ge(wT_ready, 2 * k + (0 if first == 0 else 1))
                    for t in range(first, first + n):
                        last = nc.tensor.transpose(psum_t[:, (t - first) * C:(t - first + 1) * C],
                                                   w_int[k][:, t * C:(t + 1) * C], ident[:, :])
                    last.then_inc(transposed, 1)
            pe.wait_ge(wT_ready, 4)
            pe.wait_ge(pads_ready, 8)

            taps = sorted(((kh, kw) for kh in range(3) for kw in range(3)), key=lambda t: t != (1, 1))

            def convolve(g, b, w, free):
                have = 0
                for j in range(CHUNKS):
                    if CHUNK_NEEDS[j] > have:
                        have = CHUNK_NEEDS[j]
                        pe.wait_ge(lo_ready, g * NP + have)
                    if not free:
                        pe.wait_ge(evac_done, g * CHUNKS + (j + 1 - CHUNKS))
                    for n, (kh, kw) in enumerate(taps):
                        r0, r1 = max(0, j * ROWS + kh - 1), min(H, (j + 1) * ROWS + kh - 1)
                        o0, o1 = (r0 - kh + 1 - j * ROWS) * W, (r1 - kh + 1 - j * ROWS) * W
                        for half in (hi, lo):
                            last = nc.tensor.matmul(rows_of(psum[:, j, o0:o1], r1 - r0), w[:, kh * 3 + kw, :],
                                                    window(half[b], r0, r1, kw - 1),
                                                    start=(n == 0 and half is hi),
                                                    stop=(n == TAPS - 1 and half is lo))
                    last.then_inc(chunk_done, 1)

            convolve(0, 0, wT[0], True)
            convolve(1, 1, wT[0], False)
            with pe.Fori(1, IMAGES // 2) as i:
                for b in range(2):
                    convolve(i * 2 + b, b, wT[0], False)
            with pe.Fori(IMAGES // 2, IMAGES) as i:
                for b in range(2):
                    convolve(i * 2 + b, b, wT[1], False)


_INS = ["x", "L0_conv_w1", "L0_conv_alpha1", "L0_conv_gamma1", "L0_conv_beta1",
        "L0_conv_w2", "L0_conv_alpha2", "L0_conv_gamma2", "L0_conv_beta2"]


def kernel(**inputs):
    import concourse.bacc as bacc
    from concourse.bass_utils import run_bass_kernel_spmd

    nc = bacc.Bacc("TRN2", target_bir_lowering=False, num_devices=1, dynamic_dma_scratch_size=1024)
    arrays, args = {}, []
    for name in _INS:
        a = np.ascontiguousarray(inputs[name])
        arrays[f"in_{name}"] = a
        args.append(nc.dram_tensor(f"in_{name}", a.shape, mybir.dt.from_np(a.dtype), kind="ExternalInput").ap())
    o = nc.dram_tensor("out", arrays["in_x"].shape, F32, kind="ExternalOutput").ap()
    residual_block(nc, *args, o)
    r = run_bass_kernel_spmd(nc, [arrays], core_ids=[0])
    return r.results[0]["out"]
```

```python
from contextlib import ExitStack

import concourse.bass as bass
import numpy as np
from concourse import mybir

F32 = mybir.dt.float32
F32R = mybir.dt.float32r
BF16 = mybir.dt.bfloat16
ALU = mybir.AluOpType
ACT = mybir.ActivationFunctionType

BN_EPS = 1e-5
Q_MIN, Q_MAX = -4.0, 3.0
ROUND = 12582912.0

SLOTS = 10
XBUFS = 4


def residual_block(nc, x, w1, alpha1, gamma1, beta1, w2, alpha2, gamma2, beta2, out):
    IMAGES, C, H, W = x.shape
    TAPS = w1.shape[2] * w1.shape[3]
    PIX = H * W
    ROWS = 8
    N = ROWS * W
    GROUPS = 2
    DIRECT0 = GROUPS * 2 * ROWS
    CHUNKS = (H - DIRECT0) // ROWS
    BANDS = 2 * GROUPS + CHUNKS
    M_BANKS = 4
    PITCH = W + 2
    LEAD = 2
    D_ROWS = H - DIRECT0 + 1
    V_ROWS = M_BANKS * ROWS
    D_PLANE = LEAD + D_ROWS * PITCH
    V_PLANE = LEAD + V_ROWS * PITCH
    RELU_PARTS = [(0, 2 * ROWS + 1), (2 * ROWS + 1, DIRECT0 + 1), (DIRECT0 + 1, H)]
    SPLITS = 2 * GROUPS + 1
    WEIGHTS = TAPS + 6
    M_WEIGHT = [9, 12, 0, 6]
    SPILL = IMAGES - SLOTS
    STEPS = 2 * IMAGES
    IN_LOOP3 = -(-SLOTS // XBUFS)
    PADS = 2 * (2 * GROUPS + 2) + 2
    LSQ_G = float(np.float32(1.0) / np.sqrt(np.float32(float(C * C * TAPS) * Q_MAX)))
    assert C == 128 and H % ROWS == 0 and IMAGES % XBUFS == 0 and SLOTS % 2 == 0 and SPILL % 2 == 0

    xi = x.rearrange("b c h w -> b c (h w)")
    oi = out.rearrange("b c h w -> b c (h w)")
    y1_dram = nc.dram_tensor("conv1_spill", (SPILL, C, PIX), F32, kind="Internal").ap()
    y2_dram = nc.dram_tensor("conv2_spill", (SPILL, C, PIX), F32, kind="Internal").ap()

    with ExitStack() as ctx:
        def sb(name, shape, dt):
            return ctx.enter_context(nc.sbuf_tensor(name, shape, dt))

        def sem(name):
            return ctx.enter_context(nc.semaphore(name))

        slots = sb("slots", [C, SLOTS, W + PIX], F32)
        wT = [sb(f"w{k + 1}T", [C, WEIGHTS, C], F32R) for k in range(2)]
        sizes = [V_PLANE] * (2 * GROUPS) + [D_PLANE] * 2 + [M_BANKS * N] + [N] * 4
        starts, size = [], 0
        for n in sizes:
            starts.append(size)
            size += (n + 7) // 8 * 8
        xstarts = [starts[0], starts[2], starts[4], starts[4] + PIX]
        size = max(size, xstarts[-1] + PIX)
        base = (nc.sbuf_base + 31) // 32 * 32
        sb("plane_arena", [C, size], F32)

        def placed(name, n, dt, start):
            return nc.alloc_sbuf_tensor_at(name, [C, n], dt, offset=base + start * 4)

        v_plane = [[placed(f"v{t}_{part}", V_PLANE, F32R, starts[2 * t + k]) for k, part in enumerate(("hi", "lo"))]
                   for t in range(GROUPS)]
        d_plane = [placed(f"d_{part}", D_PLANE, F32R, starts[4 + k]) for k, part in enumerate(("hi", "lo"))]
        v_rows = placed("v_rows", M_BANKS * N, F32, starts[6])
        m1 = [placed(f"m1_{t}", N, F32, starts[7 + t]) for t in range(GROUPS)]
        m_sum = placed("m_sum", N, F32, starts[9])
        m_diff = placed("m_diff", N, F32, starts[10])
        xbuf = [placed(f"xbuf{b}", PIX, F32, xstarts[b]) for b in range(XBUFS)]
        ident = sb("ident", [C, C], BF16)
        alpha_in = sb("alpha_in", [C, 2], F32)
        gb = sb("gamma_beta", [C, 4], F32)
        alpha = sb("alpha_s", [C, 2], F32)
        tiny = sb("tiny", [C, 16], F32)
        minus_half = sb("minus_half", [C, 1], F32)
        affine = sb("affine", [C, 2, 2], F32)
        chunk_stats = sb("chunk_stats", [C, BANDS, 6], F32)
        pixels = sb("pixels", [C, 1], F32)
        image_mv = sb("image_mv", [C, 2], F32)
        image_stats = sb("image_stats", [C, 2, IMAGES, 3], F32)
        total_mv = sb("total_mv", [C, 2], F32)
        psum = ctx.enter_context(nc.psum_tensor("conv_psum", [C, 8, 512], F32))
        GROUP_BANK = [0, 4]
        CHUNK_BANK = [3, 2, 7]

        w_raw = [slots[:, SLOTS - 1, W + k * C * TAPS:W + (k + 1) * C * TAPS] for k in range(2)]
        w_int = [slots[:, SLOTS - 2, W + k * C * WEIGHTS // 2:W + (k + 1) * C * WEIGHTS // 2].bitcast(BF16)
                 for k in range(2)]

        w_landed = [sem("w1_landed"), sem("w2_landed")]
        small_landed = sem("small_landed")
        ident_zeroed = sem("ident_zeroed")
        ident_ready = sem("ident_ready")
        half_ready = sem("half_ready")
        pads_ready = sem("pads_ready")
        dve_step = sem("dve_step")
        w_int_ready = sem("w_int_ready")
        transposed = sem("transposed")
        wT_ready = sem("wT_ready")
        x_landed = [sem(f"x_landed{b}") for b in range(2)]
        y1_landed = [sem(f"y1_landed{b}") for b in range(2)]
        y1_stored = [sem(f"y1_stored{b}") for b in range(2)]
        y2_stored = [sem(f"y2_stored{b}") for b in range(2)]
        hi_ready = sem("hi_ready")
        relu_ready = sem("relu_ready")
        lo_ready = sem("lo_ready")
        v_ready = sem("v_ready")
        m_done = sem("m_done")
        m1_ready = sem("m1_ready")
        sums_ready = sem("sums_ready")
        rows_ready = sem("rows_ready")
        chunk_done = sem("chunk_done")
        evac_done = sem("evac_done")
        bn_done = sem("bn_done")
        aggregated = sem("aggregated")
        image_done = sem("image_done")
        powed = sem("powed")
        var_ready = sem("var_ready")
        affine_ready = sem("affine_ready")
        res_landed = [sem(f"res_landed{b}") for b in range(XBUFS)]
        y2_landed = [sem(f"y2_landed{b}") for b in range(XBUFS)]
        added = sem("added")
        final_ready = sem("final_ready")
        out_stored = [sem(f"out_stored{b}") for b in range(XBUFS)]

        def slot(p, r0=0, r1=H):
            a, b = (r0 + 1) * W, (r1 + 1) * W
            if isinstance(p, int):
                return slots[:, p % SLOTS, a:b]
            return slots[:, bass.ds(p % SLOTS, 1), a:b].rearrange("c s n -> c (s n)")

        def every_other(p, r0):
            return slot(p, r0, r0 + 2 * ROWS).rearrange("c (r two w) -> c r two w", two=2, w=W)[:, :, 0, :]

        def dram_image(t, i):
            if isinstance(i, int):
                return t[i]
            return t[bass.ds(i, 1)].rearrange("b c n -> c (b n)")

        def rows_of(ap):
            return ap.rearrange("c (r w) -> c r w", w=W)

        def window(plane, r0, r1, shift=0):
            at = LEAD - 2 if shift < 0 else LEAD
            end = plane.shape[1] - (LEAD - at)
            rows = plane[:, at:end].rearrange("c (r w) -> c r w", w=PITCH)
            col = LEAD - at + shift
            return rows[:, r0:r1, col:col + W]

        W_LOTS = [(0, 8), (8, WEIGHTS)]

        def w_bank(k, h):
            return psum[:, 2 * k + h, :].bitcast(BF16)

        block = ctx.enter_context(nc.Block())

        @block.sync
        def _(sp):
            def load_x(g, b):
                sp.dma_start(slot(g), dram_image(xi, g)).then_inc(x_landed[b], 16)

            def split_over(g):
                sp.wait_ge(lo_ready, g * SPLITS + SPLITS)

            def step_over(g):
                sp.wait_ge(bn_done, g * BANDS + BANDS)

            sp.dma_start(w_raw[0], w1.rearrange("o c a b -> o (c a b)")).then_inc(w_landed[0], 16)
            load_x(0, 0)
            sp.dma_start(w_raw[1], w2.rearrange("o c a b -> o (c a b)")).then_inc(w_landed[1], 16)
            load_x(1, 1)

            def phase1_load(k, b, reuse):
                split_over(k)
                if reuse:
                    old = k + 2 - SLOTS
                    step_over(old)
                    sp.wait_ge(y1_stored[b], half(old) * 16 + 16)
                load_x(k + 2, b)

            def half(v):
                return v // 2

            def phase1_store(k, b, first=False):
                step_over(k)
                if not first:
                    sp.wait_ge(y1_stored[b], half(k) * 16)
                sp.dma_start(dram_image(y1_dram, k), slot(k)).then_inc(y1_stored[b], 16)

            for b in range(2):
                phase1_load(b, b, False)
                phase1_store(b, b, first=True)
            with sp.Fori(1, (SLOTS - 2) // 2) as i:
                for b in range(2):
                    phase1_load(i * 2 + b, b, False)
                    phase1_store(i * 2 + b, b)
            with sp.Fori((SLOTS - 2) // 2, SPILL // 2) as i:
                for b in range(2):
                    phase1_load(i * 2 + b, b, True)
                    phase1_store(i * 2 + b, b)
            with sp.Fori(SPILL // 2, (IMAGES - 2) // 2) as i:
                for b in range(2):
                    phase1_load(i * 2 + b, b, True)
            for b in range(2):
                sp.wait_ge(y1_stored[b], 16 * (SPILL // 2))

            def phase2_load(m, b):
                split_over(IMAGES + m - 2)
                step_over(IMAGES + m - SLOTS)
                sp.wait_ge(y2_stored[b], half(m - SLOTS) * 16 + 16)
                sp.dma_start(slot(SPILL + m), dram_image(y1_dram, m - SLOTS)).then_inc(y1_landed[b], 16)

            def phase2_store(m, b, first=False):
                step_over(IMAGES + m)
                if not first:
                    sp.wait_ge(y2_stored[b], half(m) * 16)
                sp.dma_start(dram_image(y2_dram, m), slot(SPILL + m)).then_inc(y2_stored[b], 16)

            for b in range(2):
                phase2_store(b, b, first=True)
            with sp.Fori(1, (SLOTS - 2) // 2) as i:
                for b in range(2):
                    phase2_store(i * 2 + b, b)
            with sp.Fori((SLOTS - 2) // 2, SPILL // 2) as i:
                for b in range(2):
                    phase2_load(i * 2 + b + 2, b)
                    phase2_store(i * 2 + b, b)
            with sp.Fori(SPILL // 2, (IMAGES - 2) // 2) as i:
                for b in range(2):
                    phase2_load(i * 2 + b + 2, b)
            for b in range(2):
                sp.wait_ge(y2_stored[b], 16 * (SPILL // 2))

            def load_residual(q, b):
                sp.dma_start(xbuf[b][:, :], dram_image(xi, (q + 2 * SPILL) % IMAGES)).then_inc(res_landed[b], 16)

            def load_y2(q, i, b):
                sp.wait_ge(out_stored[(b - SLOTS) % XBUFS], (q - SLOTS) // XBUFS * 16 + 16)
                sp.dma_start(slot(q + 2 * SPILL), dram_image(y2_dram, q - SLOTS)).then_inc(y2_landed[b], 16)

            last_step = STEPS - 1
            sp.wait_ge(m_done, last_step * 8 + 4)
            load_residual(0, 0)
            sp.wait_ge(m_done, last_step * 8 + 8)
            load_residual(1, 1)
            sp.wait_ge(chunk_done, STEPS * CHUNKS)
            sp.wait_ge(rows_ready, STEPS * 2 * GROUPS)
            load_residual(2, 2)
            load_residual(3, 3)

            def phase3_load(q, i, b, spilled):
                sp.wait_ge(added, q + (1 - XBUFS))
                load_residual(q, b)
                if spilled:
                    load_y2(q, i, b)

            with sp.Fori(1, SLOTS // XBUFS) as i:
                for b in range(XBUFS):
                    phase3_load(i * XBUFS + b, i, b, False)
            for q in range(SLOTS // XBUFS * XBUFS, IN_LOOP3 * XBUFS):
                phase3_load(q, q // XBUFS, q % XBUFS, q >= SLOTS)
            with sp.Fori(IN_LOOP3, IMAGES // XBUFS) as i:
                for b in range(XBUFS):
                    phase3_load(i * XBUFS + b, i, b, True)
            for b in range(XBUFS):
                sp.wait_ge(out_stored[b], 16 * (IMAGES // XBUFS))

        @block.gpsimd
        def _(pool):
            nc.gpsimd.memset(minus_half[:, :], -0.5).then_inc(half_ready, 1)
            nc.gpsimd.memset(ident[:, :], 0.0).then_inc(ident_zeroed, 1)
            pool.wait_ge(ident_zeroed, 1)
            nc.gpsimd.affine_select(out=ident[:, :], in_=ident[:, :], compare_op=ALU.not_equal, fill=1.0, base=0,
                                    pattern=[[-1, C]], channel_multiplier=1).then_inc(ident_ready, 1)
            pool.wait_ge(half_ready, 1)
            for k in range(2):
                pool.wait_ge(var_ready, k + 1)
                nc.gpsimd.tensor_tensor(tiny[:, 1:2], tiny[:, 0:1], minus_half[:, :], ALU.pow).then_inc(powed, 1)

        @block.scalar
        def _(act):
            for k, a in enumerate((alpha1, alpha2)):
                act.dma_start(alpha_in[:, k:k + 1], a.rearrange("(a n) -> a n", a=1).to_broadcast([C, 1])
                              ).then_inc(small_landed, 16)
            for k, v in enumerate((gamma1, beta1, gamma2, beta2)):
                act.dma_start(gb[:, k:k + 1], v.rearrange("(c n) -> c n", n=1)).then_inc(small_landed, 16)

            for k in range(2):
                for h, (first, end) in enumerate(W_LOTS):
                    act.wait_ge(transposed, 2 * k + h + 1)
                    nc.scalar.copy(wT[k][:, first:end, :],
                                   w_bank(k, h)[:, 0:(end - first) * C].rearrange("c (t o) -> c t o", o=C)
                                   ).then_inc(wT_ready, 1)

            def hi_group(g, t):
                for k in range(2):
                    act.wait_ge(v_ready, g * 8 + (4 * t + 2 * k + 2))
                    nc.scalar.copy(window(v_plane[t][0], 2 * k * ROWS, (2 * k + 2) * ROWS),
                                   rows_of(v_rows[:, 2 * k * N:(2 * k + 2) * N])).then_inc(hi_ready, 1)

            def hi_direct(g, p):
                if not (isinstance(g, int) and g == 0):
                    act.wait_ge(chunk_done, g * CHUNKS)
                nc.scalar.copy(window(d_plane[0], 0, D_ROWS),
                               rows_of(slot(p + SLOTS, DIRECT0 - 1))).then_inc(hi_ready, 1)

            def take_m1(g, t):
                act.wait_ge(m_done, g * 8 + (4 * t + 1))
                nc.scalar.copy(m1[t][:, :], psum[:, GROUP_BANK[t], 0:N]).then_inc(m1_ready, 1)

            def take_chunk(g, p, j):
                act.wait_ge(chunk_done, g * CHUNKS + (j + 1))
                nc.scalar.copy(slot(p + SLOTS, DIRECT0 + j * ROWS, DIRECT0 + (j + 1) * ROWS),
                               psum[:, CHUNK_BANK[j], 0:N]).then_inc(evac_done, 1)

            def relu(m, part):
                y = slot(m + SPILL, *RELU_PARTS[part])
                nc.scalar.activation(y, y, ACT.Relu, bias=affine[:, 0, 1:2],
                                     scale=affine[:, 0, 0:1]).then_inc(relu_ready, 1)

            def phase1(n, b, last=False):
                hi_direct(n, n)
                take_m1(n, 0)
                take_m1(n, 1)
                if not last:
                    hi_group(n + 1, 0)
                take_chunk(n, n, 0)
                take_chunk(n, n, 1)
                if not last:
                    hi_group(n + 1, 1)
                take_chunk(n, n, 2)

            act.wait_ge(x_landed[0], 16)
            hi_group(0, 0)
            hi_group(0, 1)
            phase1(0, 0)
            phase1(1, 1)
            with act.Fori(1, (IMAGES - 2) // 2) as i:
                for b in range(2):
                    phase1(i * 2 + b, b)
            phase1(IMAGES - 2, 0)
            phase1(IMAGES - 1, 1, last=True)

            def phase2(m, b, last=False, next_landed=False):
                g, p = m + IMAGES, m + SPILL
                act.wait_ge(relu_ready, m * 3 + 3)
                hi_direct(g, p)
                take_m1(g, 0)
                if not last:
                    if next_landed:
                        act.wait_ge(y1_landed[1 - b], (m + (1 - SLOTS)) // 2 * 16 + 16)
                    relu(m + 1, 0)
                    relu(m + 1, 1)
                take_m1(g, 1)
                if not last:
                    hi_group(g + 1, 0)
                    relu(m + 1, 2)
                take_chunk(g, p, 0)
                take_chunk(g, p, 1)
                if not last:
                    hi_group(g + 1, 1)
                take_chunk(g, p, 2)

            act.wait_ge(affine_ready, 1)
            for part in range(3):
                relu(0, part)
            hi_group(IMAGES, 0)
            hi_group(IMAGES, 1)
            with act.Fori(0, (SLOTS - 2) // 2) as i:
                for b in range(2):
                    phase2(i * 2 + b, b)
            phase2(SLOTS - 2, 0)
            phase2(SLOTS - 1, 1, next_landed=True)
            with act.Fori(SLOTS // 2, (IMAGES - 2) // 2) as i:
                for b in range(2):
                    phase2(i * 2 + b, b, next_landed=True)
            phase2(IMAGES - 2, 0, next_landed=True)
            phase2(IMAGES - 1, 1, last=True)

            act.wait_ge(affine_ready, 2)

            def finish(q, b, first=False):
                act.wait_ge(added, q + 1)
                z = slot(q + 2 * SPILL)
                nc.scalar.activation(z, z, ACT.Relu, bias=affine[:, 1, 1:2]).then_inc(final_ready, 1)
                act.wait_ge(final_ready, q + 1)
                if not first:
                    act.wait_ge(out_stored[b], q // XBUFS * 16)
                act.dma_start(dram_image(oi, (q + 2 * SPILL) % IMAGES), z).then_inc(out_stored[b], 16)

            for b in range(XBUFS):
                finish(b, b, first=True)
            with act.Fori(1, IMAGES // XBUFS) as i:
                for b in range(XBUFS):
                    finish(i * XBUFS + b, b)

        @block.vector
        def _(dve):
            steps = [0]

            def link(ins):
                steps[0] += 1
                ins.then_inc(dve_step, 1)
                dve.wait_ge(dve_step, steps[0])

            for plane in (*v_plane[0], *v_plane[1], *d_plane):
                nc.vector.memset(plane[:, 0:LEAD].bitcast(F32), 0.0).then_inc(pads_ready, 1)
                nc.vector.memset(plane[:, LEAD:].rearrange("c (r w) -> c r w", w=PITCH)[:, :, W:PITCH].bitcast(F32),
                                 0.0).then_inc(pads_ready, 1)
            nc.vector.memset(slots[:, :, 0:W], 0.0).then_inc(pads_ready, 1)
            nc.vector.memset(pixels[:, :], float(PIX)).then_inc(pads_ready, 1)

            dve.wait_ge(small_landed, 6 * 16)
            link(nc.vector.tensor_scalar(tiny[:, 4:6], alpha_in[:, :], LSQ_G, None, ALU.mult))
            link(nc.vector.tensor_tensor(tiny[:, 6:8], alpha_in[:, :], tiny[:, 4:6], ALU.subtract))
            link(nc.vector.tensor_tensor(alpha[:, :], tiny[:, 4:6], tiny[:, 6:8], ALU.add))
            link(nc.vector.reciprocal(tiny[:, 2:4], alpha[:, :]))
            for k in range(2):
                dve.wait_ge(w_landed[k], 16)
                link(nc.vector.tensor_scalar(w_raw[k], w_raw[k], tiny[:, 2 + k:3 + k], Q_MAX, ALU.mult, ALU.min))
                link(nc.vector.tensor_scalar(w_raw[k], w_raw[k], Q_MIN, ROUND, ALU.max, ALU.add))
                taps = w_int[k][:, 0:TAPS * C]
                link(nc.vector.tensor_scalar(taps.rearrange("o (t c) -> o c t", t=TAPS),
                                             w_raw[k].rearrange("o (c t) -> o c t", t=TAPS),
                                             ROUND, None, ALU.subtract))
                g0, g1, g2 = (w_int[k][:, kh * 3 * C:(kh + 1) * 3 * C] for kh in range(3))
                plus, minus = w_int[k][:, 9 * C:12 * C], w_int[k][:, 12 * C:15 * C]
                link(nc.vector.tensor_tensor(minus, g0, g2, ALU.add))
                link(nc.vector.tensor_tensor(plus, minus, g1, ALU.add))
                link(nc.vector.tensor_tensor(minus, minus, g1, ALU.subtract))
                nc.vector.tensor_scalar(w_int[k][:, 9 * C:15 * C], w_int[k][:, 9 * C:15 * C], 0.5, None,
                                        ALU.mult).then_inc(w_int_ready, 1)

            def at_least(semaphore, count):
                if not (isinstance(count, int) and count == 0):
                    dve.wait_ge(semaphore, count)

            def make_v(g, p, t):
                at_least(lo_ready, g * SPLITS + 2 * t)
                first = t * 2 * ROWS
                d0, d1, d2, d3 = (every_other(p, first + k - 1) for k in range(4))
                for k, (a, b, op) in enumerate(((d1, d2, ALU.add), (d2, d1, ALU.subtract),
                                                (d0, d2, ALU.subtract), (d3, d1, ALU.subtract))):
                    nc.vector.tensor_tensor(rows_of(v_rows[:, k * N:(k + 1) * N]), a, b, op).then_inc(v_ready, 1)

            def lo_group(g, t):
                for k in range(2):
                    dve.wait_ge(hi_ready, g * SPLITS + (2 * t + k + 1))
                    rows = 2 * k * ROWS, (2 * k + 2) * ROWS
                    nc.vector.tensor_tensor(window(v_plane[t][1], *rows), rows_of(v_rows[:, 2 * k * N:(2 * k + 2) * N]),
                                            window(v_plane[t][0], *rows).bitcast(F32),
                                            ALU.subtract).then_inc(lo_ready, 1)

            def lo_direct(g, p):
                dve.wait_ge(hi_ready, g * SPLITS + SPLITS)
                nc.vector.tensor_tensor(window(d_plane[1], 0, D_ROWS), rows_of(slot(p, DIRECT0 - 1)),
                                        window(d_plane[0], 0, D_ROWS).bitcast(F32),
                                        ALU.subtract).then_inc(lo_ready, 1)

            def take_group(g, p, t):
                bank = GROUP_BANK[t]
                m2, m0, m3 = (psum[:, bank + k, 0:N] for k in (1, 2, 3))
                at_least(rows_ready, g * 4 + 2 * t)
                dve.wait_ge(m1_ready, g * 2 + (t + 1))
                dve.wait_ge(m_done, g * 8 + (4 * t + 2))
                nc.vector.tensor_tensor(m_sum[:, :], m2, m1[t][:, :], ALU.add).then_inc(sums_ready, 1)
                nc.vector.tensor_tensor(m_diff[:, :], m1[t][:, :], m2, ALU.subtract).then_inc(sums_ready, 1)
                for k, (m, s) in enumerate(((m0, m_sum), (m3, m_diff))):
                    dve.wait_ge(m_done, g * 8 + (4 * t + 3 + k))
                    dve.wait_ge(sums_ready, g * 4 + (2 * t + 1 + k))
                    nc.vector.tensor_tensor(every_other(p, t * 2 * ROWS + k), rows_of(m), rows_of(s[:, :]),
                                            ALU.add).then_inc(rows_ready, 1)

            def group_statistics(g, p, t):
                if t == 0:
                    at_least(aggregated, g)
                for k in range(2):
                    dve.wait_ge(rows_ready, g * 4 + (2 * t + 1 + k))
                    nc.vector.bn_stats(chunk_stats[:, 2 * t + k, :], every_other(p + SLOTS, t * 2 * ROWS + k)
                                       ).then_inc(bn_done, 1)

            def chunk_statistics(g, p):
                for j in range(CHUNKS):
                    dve.wait_ge(evac_done, g * CHUNKS + (j + 1))
                    nc.vector.bn_stats(chunk_stats[:, 2 * GROUPS + j, :],
                                       slot(p + SLOTS, DIRECT0 + j * ROWS, DIRECT0 + (j + 1) * ROWS)
                                       ).then_inc(bn_done, 1)

            def image_statistics(g, phase, n):
                st = image_stats[:, phase, n:n + 1, :] if isinstance(n, int) else image_stats[:, phase, bass.ds(n, 1), :]
                at_least(image_done, g * 3)
                dve.wait_ge(bn_done, g * BANDS + BANDS)
                nc.vector.tensor_scalar(st[:, :, 0], pixels[:, :], 1.0, None, ALU.mult).then_inc(image_done, 1)
                nc.vector.bn_aggr(image_mv[:, :], chunk_stats[:, :, :]).then_inc(aggregated, 1)
                dve.wait_ge(aggregated, g + 1)
                nc.vector.tensor_scalar(st[:, :, 1], image_mv[:, 0:1], 1.0, None, ALU.mult).then_inc(image_done, 1)
                nc.vector.tensor_scalar(st[:, :, 2], image_mv[:, 1:2], float(PIX), None,
                                        ALU.mult).then_inc(image_done, 1)

            def step(g, p, phase, n, input_ready):
                lo_direct(g, p)
                take_group(g, p, 0)
                if input_ready is not None:
                    input_ready(0)
                    make_v(g + 1, p + 1, 0)
                    lo_group(g + 1, 0)
                take_group(g, p, 1)
                group_statistics(g, p, 0)
                group_statistics(g, p, 1)
                if input_ready is not None:
                    input_ready(1)
                    make_v(g + 1, p + 1, 1)
                    lo_group(g + 1, 1)
                chunk_statistics(g, p)
                image_statistics(g, phase, n)

            def batchnorm_affine(phase):
                dve.wait_ge(image_done, 3 * IMAGES * (phase + 1))
                link(nc.vector.bn_aggr(total_mv[:, :], image_stats[:, phase, :, :]))
                al, gm, be = alpha[:, phase:phase + 1], gb[:, 2 * phase:2 * phase + 1], gb[:, 2 * phase + 1:2 * phase + 2]
                link(nc.vector.tensor_scalar(tiny[:, 8:9], total_mv[:, 1:2], al, al, ALU.mult, ALU.mult))
                nc.vector.tensor_scalar(tiny[:, 0:1], tiny[:, 8:9], BN_EPS, None, ALU.add).then_inc(var_ready, 1)
                dve.wait_ge(powed, phase + 1)
                r, v = tiny[:, 1:2], tiny[:, 0:1]
                link(nc.vector.tensor_scalar(tiny[:, 9:10], r, r, v, ALU.mult, ALU.mult))
                link(nc.vector.tensor_scalar(tiny[:, 10:11], tiny[:, 9:10], -0.5, 1.5, ALU.mult, ALU.add))
                link(nc.vector.tensor_scalar(tiny[:, 11:12], tiny[:, 10:11], r, al, ALU.mult, ALU.mult))
                link(nc.vector.tensor_scalar(affine[:, phase, 0:1], tiny[:, 11:12], gm, None, ALU.mult))
                link(nc.vector.tensor_scalar(tiny[:, 12:13], affine[:, phase, 0:1], -1.0, None, ALU.mult))
                nc.vector.tensor_scalar(affine[:, phase, 1:2], total_mv[:, 0:1], tiny[:, 12:13], be,
                                        ALU.mult, ALU.add).then_inc(affine_ready, 1)

            def phase1(n, b, last=False):
                def x_ready(t):
                    if t == 0:
                        dve.wait_ge(x_landed[1 - b], (n + 1) // 2 * 16 + 16)
                step(n, n, 0, n, None if last else x_ready)

            dve.wait_ge(pads_ready, PADS)
            dve.wait_ge(x_landed[0], 16)
            for t in range(GROUPS):
                make_v(0, 0, t)
                lo_group(0, t)
            phase1(0, 0)
            phase1(1, 1)
            with dve.Fori(1, (IMAGES - 2) // 2) as i:
                for b in range(2):
                    phase1(i * 2 + b, b)
            phase1(IMAGES - 2, 0)
            phase1(IMAGES - 1, 1, last=True)
            batchnorm_affine(0)

            def phase2(m, b, last=False):
                def relu_over(t):
                    dve.wait_ge(relu_ready, m * 3 + (t + 4))
                step(m + IMAGES, m + SPILL, 1, m, None if last else relu_over)

            for t in range(GROUPS):
                dve.wait_ge(relu_ready, t + 1)
                make_v(IMAGES, SPILL, t)
                lo_group(IMAGES, t)
            with dve.Fori(0, (IMAGES - 2) // 2) as i:
                for b in range(2):
                    phase2(i * 2 + b, b)
            phase2(IMAGES - 2, 0)
            phase2(IMAGES - 1, 1, last=True)
            batchnorm_affine(1)
            dve.wait_ge(affine_ready, 2)

            def add_residual(q, i, b, spilled):
                dve.wait_ge(res_landed[b], i * 16 + 16)
                if spilled:
                    dve.wait_ge(y2_landed[b], (i - (-(-(SLOTS - b) // XBUFS) - 1)) * 16)
                z = slot(q + 2 * SPILL)
                nc.vector.scalar_tensor_tensor(out=z, in0=z, scalar=affine[:, 1, 0:1], in1=xbuf[b][:, :],
                                               op0=ALU.mult, op1=ALU.add).then_inc(added, 1)

            with dve.Fori(0, SLOTS // XBUFS) as i:
                for b in range(XBUFS):
                    add_residual(i * XBUFS + b, i, b, False)
            for q in range(SLOTS // XBUFS * XBUFS, IN_LOOP3 * XBUFS):
                add_residual(q, q // XBUFS, q % XBUFS, q >= SLOTS)
            with dve.Fori(IN_LOOP3, IMAGES // XBUFS) as i:
                for b in range(XBUFS):
                    add_residual(i * XBUFS + b, i, b, True)

        @block.tensor
        def _(pe):
            pe.wait_ge(ident_ready, 1)
            for k in range(2):
                pe.wait_ge(w_int_ready, k + 1)
                for h, (first, end) in enumerate(W_LOTS):
                    for t in range(first, end):
                        last = nc.tensor.transpose(w_bank(k, h)[:, (t - first) * C:(t - first + 1) * C],
                                                   w_int[k][:, t * C:(t + 1) * C], ident[:, :])
                    last.then_inc(transposed, 1)
            pe.wait_ge(wT_ready, 4)
            pe.wait_ge(pads_ready, PADS)

            def group(g, t, w, first_step):
                if not first_step:
                    pe.wait_ge(evac_done, g * CHUNKS - CHUNKS + (2 if t == 0 else 3))
                for k in range(M_BANKS):
                    if k % 2 == 0:
                        pe.wait_ge(lo_ready, g * SPLITS + (2 * t + k // 2 + 1))
                    for kw in range(3):
                        for half in range(2):
                            last = nc.tensor.matmul(rows_of(psum[:, GROUP_BANK[t] + k, 0:N]),
                                                    w[:, M_WEIGHT[k] + kw, :],
                                                    window(v_plane[t][half], k * ROWS, (k + 1) * ROWS, kw - 1),
                                                    start=(kw == 0 and half == 0), stop=(kw == 2 and half == 1))
                    last.then_inc(m_done, 1)

            taps = sorted(((kh, kw) for kh in range(3) for kw in range(3)), key=lambda t: t != (1, 1))

            def chunk(g, j, w):
                if j == 0:
                    pe.wait_ge(lo_ready, g * SPLITS + SPLITS)
                pe.wait_ge(rows_ready, g * 4 + (2 if CHUNK_BANK[j] < 4 else 4))
                for n, (kh, kw) in enumerate(taps):
                    first = DIRECT0 + j * ROWS + kh - 1
                    r0, r1 = first, min(H, first + ROWS)
                    for half in range(2):
                        last = nc.tensor.matmul(rows_of(psum[:, CHUNK_BANK[j], 0:(r1 - r0) * W]),
                                                w[:, kh * 3 + kw, :],
                                                window(d_plane[half], r0 - DIRECT0 + 1, r1 - DIRECT0 + 1, kw - 1),
                                                start=(n == 0 and half == 0), stop=(n == TAPS - 1 and half == 1))
                last.then_inc(chunk_done, 1)

            def convolve(g, w, first_step=False):
                for t in range(GROUPS):
                    group(g, t, w, first_step)
                for j in range(CHUNKS):
                    chunk(g, j, w)

            convolve(0, wT[0], first_step=True)
            convolve(1, wT[0])
            with pe.Fori(1, IMAGES // 2) as i:
                for b in range(2):
                    convolve(i * 2 + b, wT[0])
            with pe.Fori(IMAGES // 2, IMAGES) as i:
                for b in range(2):
                    convolve(i * 2 + b, wT[1])


_INS = ["x", "L0_conv_w1", "L0_conv_alpha1", "L0_conv_gamma1", "L0_conv_beta1",
        "L0_conv_w2", "L0_conv_alpha2", "L0_conv_gamma2", "L0_conv_beta2"]


def kernel(**inputs):
    import concourse.bacc as bacc
    from concourse.bass_utils import run_bass_kernel_spmd

    nc = bacc.Bacc("TRN2", target_bir_lowering=False, num_devices=1, dynamic_dma_scratch_size=1024)
    arrays, args = {}, []
    for name in _INS:
        a = np.ascontiguousarray(inputs[name])
        arrays[f"in_{name}"] = a
        args.append(nc.dram_tensor(f"in_{name}", a.shape, mybir.dt.from_np(a.dtype), kind="ExternalInput").ap())
    o = nc.dram_tensor("out", arrays["in_x"].shape, F32, kind="ExternalOutput").ap()
    residual_block(nc, *args, o)
    r = run_bass_kernel_spmd(nc, [arrays], core_ids=[0])
    return r.results[0]["out"]
```

```python
from contextlib import ExitStack

import concourse.bass as bass
import numpy as np
from concourse import mybir

F32 = mybir.dt.float32
F32R = mybir.dt.float32r
BF16 = mybir.dt.bfloat16
ALU = mybir.AluOpType
ACT = mybir.ActivationFunctionType

BN_EPS = 1e-5
Q_MIN, Q_MAX = -4.0, 3.0
ROUND = 12582912.0

SLOTS = 12
XBUFS = 5


def residual_block(nc, x, w1, alpha1, gamma1, beta1, w2, alpha2, gamma2, beta2, out):
    IMAGES, C, H, W = x.shape
    TAPS = w1.shape[2] * w1.shape[3]
    PIX = H * W
    GROUPS = 2
    PAIRS = 9
    N = PAIRS * W
    DIRECT0 = GROUPS * 2 * PAIRS
    CHUNKS = [(36, 43), (43, 50), (50, 56)]
    NC = len(CHUNKS)
    M_BANKS = 4
    PITCH = W + 2
    LEAD = 2
    D_ROWS = H - DIRECT0 + 1
    V_ROWS = M_BANKS * PAIRS
    V_OPS = 3
    D_PLANE = LEAD + D_ROWS * PITCH
    V_PLANE = LEAD + V_ROWS * PITCH
    RELU_PARTS = [(0, 2 * PAIRS + 1), (2 * PAIRS + 1, DIRECT0 + 1), (DIRECT0 + 1, H)]
    SPLITS = 2 * GROUPS + 1
    WEIGHTS = TAPS + 6
    M_WEIGHT = [9, 12, 0, 6]
    SQUARES = [(0, 2 * PAIRS), (2 * PAIRS, DIRECT0), (DIRECT0, CHUNKS[-1][0]), CHUNKS[-1]]
    NSQ = len(SQUARES)
    SUM_COLS = 2 * GROUPS + NC
    COLS = SUM_COLS + len(SQUARES)
    SPILL = IMAGES - SLOTS
    STEPS = 2 * IMAGES
    OWN_LOTS = SLOTS // XBUFS
    DRAM_LOT = -(-SLOTS // XBUFS)
    LOTS = IMAGES // XBUFS
    PADS = 2 * (2 * GROUPS + 2)
    LSQ_G = float(np.float32(1.0) / np.sqrt(np.float32(float(C * C * TAPS) * Q_MAX)))
    assert C == 128 and CHUNKS[0][0] == DIRECT0 and CHUNKS[-1][1] == H and SLOTS % 2 == 0 and SPILL % 2 == 0

    xi = x.rearrange("b c h w -> b c (h w)")
    oi = out.rearrange("b c h w -> b c (h w)")
    y1_dram = nc.dram_tensor("conv1_spill", (SPILL, C, PIX), F32, kind="Internal").ap()
    y2_dram = nc.dram_tensor("conv2_spill", (SPILL, C, PIX), F32, kind="Internal").ap()

    with ExitStack() as ctx:
        def sb(name, shape, dt):
            return ctx.enter_context(nc.sbuf_tensor(name, shape, dt))

        def sem(name):
            return ctx.enter_context(nc.semaphore(name))

        slots = sb("slots", [C, SLOTS, W + PIX], F32)
        sizes = [WEIGHTS * C, M_BANKS * N] + [V_PLANE] * (2 * GROUPS) + [N] * 2 + [D_PLANE] * 2
        starts, size = [], 0
        for n in sizes:
            starts.append(size)
            size += (n + 7) // 8 * 8
        size = max(size, XBUFS * PIX)
        assert PIX <= starts[2] and 2 * PIX <= starts[4] and 3 * PIX <= starts[6] and 4 * PIX <= starts[7]
        base = (nc.sbuf_base + 31) // 32 * 32
        sb("plane_arena", [C, size], F32)

        def placed(name, n, dt, start):
            return nc.alloc_sbuf_tensor_at(name, [C, n], dt, offset=base + start * 4)

        w1T = nc.alloc_sbuf_tensor_at("w1T", [C, WEIGHTS, C], F32R, offset=base + starts[0] * 4)
        wT = [w1T, sb("w2T", [C, WEIGHTS, C], F32R)]

        HALVES = list(enumerate(("hi", "lo")))
        v_plane = [[placed(f"v{t}_{part}", V_PLANE, F32R, starts[2 + 2 * t + k]) for k, part in HALVES]
                   for t in range(GROUPS)]
        d_plane = [placed(f"d_{part}", D_PLANE, F32R, starts[8 + k]) for k, part in HALVES]
        v_rows = placed("v_rows", M_BANKS * N, F32, starts[1])
        m1 = placed("m1", N, F32, starts[6])
        m_sum = placed("m_sum", N, F32, starts[7])
        xbuf = [placed(f"xbuf{b}", PIX, F32, b * PIX) for b in range(XBUFS)]
        ident = sb("ident", [C, C], BF16)
        alpha_in = sb("alpha_in", [C, 2], F32)
        gb = sb("gamma_beta", [C, 4], F32)
        alpha = sb("alpha_s", [C, 2], F32)
        alpha_squared = sb("alpha_squared", [C, 2], F32)
        tiny = sb("tiny", [C, 16], F32)
        minus_half = sb("minus_half", [C, 1], F32)
        affine = sb("affine", [C, 2, 2], F32)
        squares = sb("squares", [C, 2 * PAIRS * W], BF16)
        sums = [sb(f"sums{b}", [C, COLS], F32) for b in range(2)]
        totals = sb("totals", [C, 2, COLS], F32)
        minus_shift = sb("minus_shift", [C, 2], F32)
        psum = ctx.enter_context(nc.psum_tensor("conv_psum", [C, 8, 512], F32))
        GROUP_BANK = [0, 4]
        CHUNK_BANK = [3, 2, 7]

        w_raw = [slots[:, SLOTS - 1, W + k * C * TAPS:W + (k + 1) * C * TAPS] for k in range(2)]
        w_int = [slots[:, SLOTS - 2, W + k * C * WEIGHTS // 2:W + (k + 1) * C * WEIGHTS // 2].bitcast(BF16)
                 for k in range(2)]

        w_landed = [sem("w1_landed"), sem("w2_landed")]
        alpha_landed = sem("alpha_landed")
        small_landed = sem("small_landed")
        x0_top_landed = sem("x0_top_landed")
        ident_zeroed = sem("ident_zeroed")
        ident_ready = sem("ident_ready")
        half_ready = sem("half_ready")
        pads_ready = sem("pads_ready")
        zeros_ready = sem("zeros_ready")
        dve_step = sem("dve_step")
        alpha_ready = sem("alpha_ready")
        pool_step = sem("pool_step")
        w_int_ready = [sem("w1_int_ready"), sem("w2_int_ready")]
        transposed = sem("transposed")
        wT_ready = sem("wT_ready")
        x_landed = [sem(f"x_landed{b}") for b in range(2)]
        y1_landed = [sem(f"y1_landed{b}") for b in range(2)]
        y1_stored = [sem(f"y1_stored{b}") for b in range(2)]
        y2_stored = [sem(f"y2_stored{b}") for b in range(2)]
        v1_hi_ready = sem("v1_hi_ready")
        v1_lo_ready = sem("v1_lo_ready")
        hi_ready = sem("hi_ready")
        relu_ready = sem("relu_ready")
        lo_ready = sem("lo_ready")
        v_ready = sem("v_ready")
        m_done = sem("m_done")
        m1_ready = sem("m1_ready")
        sums_ready = sem("sums_ready")
        rows_ready = sem("rows_ready")
        chunk_done = sem("chunk_done")
        evac_done = sem("evac_done")
        squared = sem("squared")
        totalled = sem("totalled")
        shift_ready = sem("shift_ready")
        powed = sem("powed")
        var_ready = sem("var_ready")
        affine_ready = sem("affine_ready")
        res_landed = [sem(f"res_landed{b}") for b in range(XBUFS)]
        y2_landed = [sem(f"y2_landed{b}") for b in range(XBUFS)]
        added = sem("added")
        final_ready = sem("final_ready")
        out_stored = [sem(f"out_stored{b}") for b in range(XBUFS)]

        def slot(p, r0=0, r1=H):
            a, b = (r0 + 1) * W, (r1 + 1) * W
            if isinstance(p, int):
                return slots[:, p % SLOTS, a:b]
            return slots[:, bass.ds(p % SLOTS, 1), a:b].rearrange("c s n -> c (s n)")

        def every_other(p, r0):
            return slot(p, r0, r0 + 2 * PAIRS).rearrange("c (r two w) -> c r two w", two=2, w=W)[:, :, 0, :]

        def dram_image(t, i):
            if isinstance(i, int):
                return t[i]
            return t[bass.ds(i, 1)].rearrange("b c n -> c (b n)")

        def rows_of(ap):
            return ap.rearrange("c (r w) -> c r w", w=W)

        def window(plane, r0, r1, shift=0):
            at = LEAD - 2 if shift < 0 else LEAD
            end = plane.shape[1] - (LEAD - at)
            rows = plane[:, at:end].rearrange("c (r w) -> c r w", w=PITCH)
            col = LEAD - at + shift
            return rows[:, r0:r1, col:col + W]

        W_LOTS = [(0, 8), (8, WEIGHTS)]
        W_BANK = [0, 5]

        def w_bank(k, h):
            return psum[:, W_BANK[k] + h, :].bitcast(BF16)

        def taps_to_integers(engine, k, link):
            link(engine.tensor_scalar(w_raw[k], w_raw[k], tiny[:, 2 + k:3 + k], Q_MAX, ALU.mult, ALU.min))
            link(engine.tensor_scalar(w_raw[k], w_raw[k], Q_MIN, ROUND, ALU.max, ALU.add))
            engine.tensor_scalar(w_int[k][:, 0:TAPS * C].rearrange("o (t c) -> o c t", t=TAPS),
                                 w_raw[k].rearrange("o (c t) -> o c t", t=TAPS),
                                 ROUND, None, ALU.subtract).then_inc(w_int_ready[k], 1)

        def sum_taps(engine, k, link):
            g0, g1, g2 = (w_int[k][:, kh * 3 * C:(kh + 1) * 3 * C] for kh in range(3))
            plus, minus = w_int[k][:, 9 * C:12 * C], w_int[k][:, 12 * C:15 * C]
            link(engine.tensor_tensor(minus, g0, g2, ALU.add))
            link(engine.tensor_tensor(plus, minus, g1, ALU.add))
            link(engine.tensor_tensor(minus, minus, g1, ALU.subtract))
            both = w_int[k][:, 9 * C:15 * C]
            engine.tensor_scalar(both, both, 0.5, None, ALU.mult).then_inc(w_int_ready[k], 1)

        def in_lots(engine, first_lot, image):
            with engine.Fori(first_lot, OWN_LOTS) as i:
                for b in range(XBUFS):
                    image(i * XBUFS + b, i, b, False)
            for q in range(OWN_LOTS * XBUFS, DRAM_LOT * XBUFS):
                image(q, q // XBUFS, q % XBUFS, q >= SLOTS)
            with engine.Fori(DRAM_LOT, LOTS) as i:
                for b in range(XBUFS):
                    image(i * XBUFS + b, i, b, True)
            for q in range(LOTS * XBUFS, IMAGES):
                image(q, q // XBUFS, q % XBUFS, True)

        block = ctx.enter_context(nc.Block())

        @block.sync
        def _(sp):
            def load_x(g, b):
                sp.dma_start(slot(g), dram_image(xi, g)).then_inc(x_landed[b], 16)

            def split_over(g):
                sp.wait_ge(lo_ready, g * SPLITS + SPLITS)

            def step_over(g):
                sp.wait_ge(squared, g * NSQ + NSQ)

            for k, a in enumerate((alpha1, alpha2)):
                sp.dma_start(alpha_in[:, k:k + 1], a.rearrange("(a n) -> a n", a=1).to_broadcast([C, 1])
                             ).then_inc(alpha_landed, 16)
            sp.dma_start(w_raw[0], w1.rearrange("o c a b -> o (c a b)")).then_inc(w_landed[0], 16)
            top = (2 * PAIRS + 1) * W
            sp.dma_start(slot(0, 0, 2 * PAIRS + 1), xi[0, :, 0:top]).then_inc(x0_top_landed, 16)
            sp.dma_start(slot(0, 2 * PAIRS + 1, H), xi[0, :, top:PIX]).then_inc(x_landed[0], 16)
            sp.dma_start(w_raw[1], w2.rearrange("o c a b -> o (c a b)")).then_inc(w_landed[1], 16)
            load_x(1, 1)

            def phase1_load(k, b, reuse):
                split_over(k)
                if reuse:
                    old = k + 2 - SLOTS
                    step_over(old)
                    sp.wait_ge(y1_stored[b], half(old) * 16 + 16)
                load_x(k + 2, b)

            def half(v):
                return v // 2

            def phase1_store(k, b, first=False):
                step_over(k)
                if not first:
                    sp.wait_ge(y1_stored[b], half(k) * 16)
                sp.dma_start(dram_image(y1_dram, k), slot(k)).then_inc(y1_stored[b], 16)

            for b in range(2):
                phase1_load(b, b, False)
                phase1_store(b, b, first=True)
            with sp.Fori(1, (SLOTS - 2) // 2) as i:
                for b in range(2):
                    phase1_load(i * 2 + b, b, False)
                    phase1_store(i * 2 + b, b)
            with sp.Fori((SLOTS - 2) // 2, SPILL // 2) as i:
                for b in range(2):
                    phase1_load(i * 2 + b, b, True)
                    phase1_store(i * 2 + b, b)
            with sp.Fori(SPILL // 2, (IMAGES - 2) // 2) as i:
                for b in range(2):
                    phase1_load(i * 2 + b, b, True)
            for b in range(2):
                sp.wait_ge(y1_stored[b], 16 * (SPILL // 2))

            def phase2_load(m, b):
                split_over(IMAGES + m - 2)
                step_over(IMAGES + m - SLOTS)
                sp.wait_ge(y2_stored[b], half(m - SLOTS) * 16 + 16)
                sp.dma_start(slot(SPILL + m), dram_image(y1_dram, m - SLOTS)).then_inc(y1_landed[b], 16)

            def phase2_store(m, b, first=False):
                step_over(IMAGES + m)
                if not first:
                    sp.wait_ge(y2_stored[b], half(m) * 16)
                sp.dma_start(dram_image(y2_dram, m), slot(SPILL + m)).then_inc(y2_stored[b], 16)

            for b in range(2):
                phase2_store(b, b, first=True)
            with sp.Fori(1, (SLOTS - 2) // 2) as i:
                for b in range(2):
                    phase2_store(i * 2 + b, b)
            with sp.Fori((SLOTS - 2) // 2, SPILL // 2) as i:
                for b in range(2):
                    phase2_load(i * 2 + b + 2, b)
                    phase2_store(i * 2 + b, b)
            with sp.Fori(SPILL // 2, (IMAGES - 2) // 2) as i:
                for b in range(2):
                    phase2_load(i * 2 + b + 2, b)
            for b in range(2):
                sp.wait_ge(y2_stored[b], 16 * (SPILL // 2))

            def load_residual(q, b):
                sp.dma_start(xbuf[b][:, :], dram_image(xi, (q + 2 * SPILL) % IMAGES)).then_inc(res_landed[b], 16)

            def load_y2(q, i, b):
                sp.wait_ge(out_stored[(b - SLOTS) % XBUFS], (i + ((b - SLOTS) // XBUFS + 1)) * 16)
                sp.dma_start(slot(q + 2 * SPILL), dram_image(y2_dram, q - SLOTS)).then_inc(y2_landed[b], 16)

            last_step = STEPS - 1
            sp.wait_ge(lo_ready, last_step * SPLITS + (SPLITS - 1))
            load_residual(0, 0)
            sp.wait_ge(m_done, last_step * 8 + 4)
            load_residual(1, 1)
            sp.wait_ge(m_done, last_step * 8 + 8)
            load_residual(2, 2)
            sp.wait_ge(rows_ready, STEPS * 2 * GROUPS)
            load_residual(3, 3)
            sp.wait_ge(chunk_done, STEPS * NC)
            load_residual(4, 4)

            def phase3_load(q, i, b, spilled):
                sp.wait_ge(added, q + (1 - XBUFS))
                load_residual(q, b)
                if spilled:
                    load_y2(q, i, b)

            in_lots(sp, 1, phase3_load)
            for b in range(XBUFS):
                sp.wait_ge(out_stored[b], 16 * len(range(b, IMAGES, XBUFS)))

        @block.gpsimd
        def _(pool):
            nc.gpsimd.memset(minus_half[:, :], -0.5).then_inc(half_ready, 1)
            nc.gpsimd.memset(ident[:, :], 0.0).then_inc(ident_zeroed, 1)
            pool.wait_ge(ident_zeroed, 1)
            nc.gpsimd.affine_select(out=ident[:, :], in_=ident[:, :], compare_op=ALU.not_equal, fill=1.0, base=0,
                                    pattern=[[-1, C]], channel_multiplier=1).then_inc(ident_ready, 1)
            for plane in (*v_plane[0], *v_plane[1], *d_plane):
                nc.gpsimd.memset(plane[:, 0:LEAD].bitcast(F32), 0.0).then_inc(pads_ready, 1)
                nc.gpsimd.memset(plane[:, LEAD:].rearrange("c (r w) -> c r w", w=PITCH)[:, :, W:PITCH].bitcast(F32),
                                 0.0).then_inc(pads_ready, 1)
            steps = [0]

            def link(ins):
                steps[0] += 1
                ins.then_inc(pool_step, 1)
                pool.wait_ge(pool_step, steps[0])

            pool.wait_ge(alpha_ready, 1)
            pool.wait_ge(w_landed[1], 16)
            taps_to_integers(nc.gpsimd, 1, link)
            pool.wait_ge(w_int_ready[1], 1)
            sum_taps(nc.gpsimd, 1, link)

            pool.wait_ge(half_ready, 1)
            for k in range(2):
                pool.wait_ge(var_ready, k + 1)
                nc.gpsimd.tensor_tensor(tiny[:, 1:2], tiny[:, 0:1], minus_half[:, :], ALU.pow).then_inc(powed, 1)

        @block.scalar
        def _(act):
            for k, v in enumerate((gamma1, beta1, gamma2, beta2)):
                act.dma_start(gb[:, k:k + 1], v.rearrange("(c n) -> c n", n=1)).then_inc(small_landed, 16)

            def take_weights(k):
                for h, (first, end) in enumerate(W_LOTS):
                    act.wait_ge(transposed, 2 * k + h + 1)
                    nc.scalar.copy(wT[k][:, first:end, :],
                                   w_bank(k, h)[:, 0:(end - first) * C].rearrange("c (t o) -> c t o", o=C)
                                   ).then_inc(wT_ready, 1)

            def hi_of_v(t, first, end):
                return nc.scalar.copy(window(v_plane[t][0], first * PAIRS, end * PAIRS),
                                      rows_of(v_rows[:, first * N:end * N]))

            def hi_group(g, t, parts=(0, 1), v1_alone=False):
                if v1_alone:
                    act.wait_ge(v_ready, g * GROUPS * V_OPS + 1)
                    hi_of_v(t, 0, 1).then_inc(v1_hi_ready, 1)
                for k in parts:
                    act.wait_ge(v_ready, g * GROUPS * V_OPS + (V_OPS * t + k + 2))
                    hi_of_v(t, 1 if v1_alone and k == 0 else 2 * k, 2 * k + 2).then_inc(hi_ready, 1)

            def hi_direct(g, p):
                if not (isinstance(g, int) and g == 0):
                    act.wait_ge(chunk_done, g * NC)
                nc.scalar.copy(window(d_plane[0], 0, D_ROWS),
                               rows_of(slot(p + SLOTS, DIRECT0 - 1))).then_inc(hi_ready, 1)

            def take_m1(g, t):
                if not (isinstance(g, int) and g == 0 and t == 0):
                    act.wait_ge(rows_ready, g * 4 + 2 * t)
                act.wait_ge(m_done, g * 8 + (4 * t + 1))
                nc.scalar.copy(m1[:, :], psum[:, GROUP_BANK[t], 0:N]).then_inc(m1_ready, 1)

            def take_chunk(g, p, b, j):
                r0, r1 = CHUNKS[j]
                col = 2 * GROUPS + j
                act.wait_ge(chunk_done, g * NC + (j + 1))
                nc.scalar.activation(slot(p + SLOTS, r0, r1), psum[:, CHUNK_BANK[j], 0:(r1 - r0) * W], ACT.Identity,
                                     accum_out=sums[b][:, col:col + 1]).then_inc(evac_done, 1)

            def square(g, p, b, phase, part):
                r0, r1 = SQUARES[part]
                if not (isinstance(g, int) and g * NSQ + part == 0):
                    act.wait_ge(squared, g * NSQ + part)
                if part < GROUPS:
                    act.wait_ge(rows_ready, g * 4 + (2 * part + 2))
                else:
                    act.wait_ge(evac_done, g * NC + (NC + part - (NSQ - 1)))
                col = SUM_COLS + part
                nc.scalar.activation(squares[:, 0:(r1 - r0) * W], slot(p + (part + 1) * SLOTS, r0, r1), ACT.Square,
                                     bias=minus_shift[:, phase:phase + 1],
                                     accum_out=sums[b][:, col:col + 1]).then_inc(squared, 1)

            def late_squares(g, p, b, phase, parts):
                act.wait_ge(shift_ready, phase + 1)
                for part in parts:
                    square(g, p, b, phase, part)

            def relu(m, part):
                y = slot(m + SPILL, *RELU_PARTS[part])
                nc.scalar.activation(y, y, ACT.Relu, bias=affine[:, 0, 1:2],
                                     scale=affine[:, 0, 0:1]).then_inc(relu_ready, 1)

            def step(g, p, b, phase, first=False, second=False, last=False, relu_next=None):
                hi_direct(g, p)
                take_m1(g, 0)
                if relu_next is not None:
                    relu_next(0)
                    relu_next(1)
                if second:
                    late_squares(g - 1, p - 1, 1 - b, phase, range(2))
                take_m1(g, 1)
                if not last:
                    hi_group(g + 1, 0)
                if second:
                    late_squares(g - 1, p - 1, 1 - b, phase, range(2, NSQ))
                if not first:
                    square(g, p, b, phase, 0)
                if relu_next is not None:
                    relu_next(2)
                take_chunk(g, p, b, 0)
                if not first:
                    square(g, p, b, phase, 1)
                take_chunk(g, p, b, 1)
                if not last:
                    hi_group(g + 1, 1)
                if not first:
                    square(g, p, b, phase, 2)
                take_chunk(g, p, b, 2)
                if not first:
                    square(g, p, b, phase, 3)

            hi_group(0, 0, parts=(0,), v1_alone=True)
            take_weights(0)
            hi_group(0, 0, parts=(1,))
            hi_group(0, 1)
            step(0, 0, 0, 0, first=True)
            step(1, 1, 1, 0, second=True)
            take_weights(1)
            with act.Fori(1, (IMAGES - 2) // 2) as i:
                for b in range(2):
                    step(i * 2 + b, i * 2 + b, b, 0)
            step(IMAGES - 2, IMAGES - 2, 0, 0)
            step(IMAGES - 1, IMAGES - 1, 1, 0, last=True)

            def phase2(m, b, first=False, second=False, last=False, next_landed=False):
                def relu_next(part):
                    if part == 0 and next_landed:
                        act.wait_ge(y1_landed[1 - b], (m + (1 - SLOTS)) // 2 * 16 + 16)
                    relu(m + 1, part)
                act.wait_ge(relu_ready, m * 3 + 3)
                step(m + IMAGES, m + SPILL, b, 1, first, second, last, None if last else relu_next)

            act.wait_ge(affine_ready, 1)
            relu(0, 0)
            hi_group(IMAGES, 0, parts=(0,), v1_alone=True)
            relu(0, 1)
            hi_group(IMAGES, 0, parts=(1,))
            relu(0, 2)
            hi_group(IMAGES, 1)
            phase2(0, 0, first=True)
            phase2(1, 1, second=True)
            with act.Fori(1, (SLOTS - 2) // 2) as i:
                for b in range(2):
                    phase2(i * 2 + b, b)
            phase2(SLOTS - 2, 0)
            phase2(SLOTS - 1, 1, next_landed=True)
            with act.Fori(SLOTS // 2, (IMAGES - 2) // 2) as i:
                for b in range(2):
                    phase2(i * 2 + b, b, next_landed=True)
            phase2(IMAGES - 2, 0, next_landed=True)
            phase2(IMAGES - 1, 1, last=True)

            act.wait_ge(affine_ready, 2)

            def finish(q, i, b, spilled):
                act.wait_ge(added, q + 1)
                z = slot(q + 2 * SPILL)
                nc.scalar.activation(z, z, ACT.Relu, bias=affine[:, 1, 1:2]).then_inc(final_ready, 1)
                act.wait_ge(final_ready, q + 1)
                if not (isinstance(i, int) and i == 0):
                    act.wait_ge(out_stored[b], i * 16)
                act.dma_start(dram_image(oi, (q + 2 * SPILL) % IMAGES), z).then_inc(out_stored[b], 16)

            for b in range(XBUFS):
                finish(b, 0, b, False)
            in_lots(act, 1, finish)

        @block.vector
        def _(dve):
            steps = [0]

            def link(ins):
                steps[0] += 1
                ins.then_inc(dve_step, 1)
                dve.wait_ge(dve_step, steps[0])

            nc.vector.memset(slots[:, :, 0:W], 0.0).then_inc(zeros_ready, 1)
            nc.vector.memset(totals[:, :, :], 0.0).then_inc(zeros_ready, 1)

            dve.wait_ge(alpha_landed, 2 * 16)
            link(nc.vector.tensor_scalar(tiny[:, 4:6], alpha_in[:, :], LSQ_G, None, ALU.mult))
            link(nc.vector.tensor_tensor(tiny[:, 6:8], alpha_in[:, :], tiny[:, 4:6], ALU.subtract))
            link(nc.vector.tensor_tensor(alpha[:, :], tiny[:, 4:6], tiny[:, 6:8], ALU.add))
            link(nc.vector.tensor_tensor(alpha_squared[:, :], alpha[:, :], alpha[:, :], ALU.mult))
            nc.vector.reciprocal(tiny[:, 2:4], alpha[:, :]).then_inc(alpha_ready, 1)
            dve.wait_ge(alpha_ready, 1)

            def at_least(semaphore, count):
                if not (isinstance(count, int) and count == 0):
                    dve.wait_ge(semaphore, count)

            def make_v(g, p, t, before_v0=None):
                at_least(lo_ready, g * SPLITS + 2 * t)
                first = t * 2 * PAIRS
                d1, d2 = every_other(p, first), every_other(p, first + 1)
                for k, op in enumerate((ALU.add, ALU.subtract)):
                    nc.vector.tensor_tensor(rows_of(v_rows[:, k * N:(k + 1) * N]), d2, d1, op).then_inc(v_ready, 1)
                if before_v0 is not None:
                    before_v0()
                above, below = (slot(p, first + k, first + k + 2 * PAIRS) for k in (-1, 1))
                nc.vector.tensor_tensor(v_rows[:, 2 * N:4 * N], below, above, ALU.subtract).then_inc(v_ready, 1)

            def lo_of_v(t, first, end):
                rows = first * PAIRS, end * PAIRS
                return nc.vector.tensor_tensor(window(v_plane[t][1], *rows), rows_of(v_rows[:, first * N:end * N]),
                                               window(v_plane[t][0], *rows).bitcast(F32), ALU.subtract)

            def lo_group(g, t, parts=(0, 1), v1_alone=False):
                for k in parts:
                    dve.wait_ge(hi_ready, g * SPLITS + (2 * t + k + 1))
                    lo_of_v(t, 1 if v1_alone and k == 0 else 2 * k, 2 * k + 2).then_inc(lo_ready, 1)

            def first_group(g, p, phase, sums=None):
                def lo_of_v1_and_v2():
                    if sums is not None:
                        sums()
                    dve.wait_ge(v1_hi_ready, phase + 1)
                    lo_of_v(0, 0, 1).then_inc(v1_lo_ready, 1)
                    lo_group(g, 0, parts=(0,), v1_alone=True)
                make_v(g, p, 0, before_v0=lo_of_v1_and_v2)
                lo_group(g, 0, parts=(1,))

            def lo_direct(g, p):
                dve.wait_ge(hi_ready, g * SPLITS + SPLITS)
                nc.vector.tensor_tensor(window(d_plane[1], 0, D_ROWS), rows_of(slot(p, DIRECT0 - 1)),
                                        window(d_plane[0], 0, D_ROWS).bitcast(F32),
                                        ALU.subtract).then_inc(lo_ready, 1)

            def take_group(g, p, b, t):
                bank = GROUP_BANK[t]
                m2, m0, m3 = (psum[:, bank + k, 0:N] for k in (1, 2, 3))
                at_least(rows_ready, g * 4 + 2 * t)
                dve.wait_ge(m1_ready, g * 2 + (t + 1))
                dve.wait_ge(m_done, g * 8 + (4 * t + 2))
                nc.vector.tensor_tensor(m_sum[:, :], m2, m1[:, :], ALU.add).then_inc(sums_ready, 1)
                dve.wait_ge(sums_ready, g * 4 + (2 * t + 1))
                nc.vector.tensor_tensor(m1[:, :], m1[:, :], m2, ALU.subtract).then_inc(sums_ready, 1)
                for k, (m, s) in enumerate(((m0, m_sum), (m3, m1))):
                    dve.wait_ge(m_done, g * 8 + (4 * t + 3 + k))
                    dve.wait_ge(sums_ready, g * 4 + (2 * t + 1 + k))
                    col = 2 * t + k
                    nc.vector.scalar_tensor_tensor(out=every_other(p, t * 2 * PAIRS + k), in0=rows_of(m),
                                                   scalar=(-1.0, 1.0)[k], in1=rows_of(s[:, :]),
                                                   op0=ALU.mult, op1=ALU.add,
                                                   accum_out=sums[b][:, col:col + 1]).then_inc(rows_ready, 1)

            def add_totals(g, b, phase):
                dve.wait_ge(squared, g * NSQ + NSQ)
                at_least(totalled, g)
                nc.vector.tensor_tensor(totals[:, phase, :], totals[:, phase, :], sums[b][:, :],
                                        ALU.add).then_inc(totalled, 1)

            def find_shift(g, phase):
                dve.wait_ge(evac_done, g * NC + NC)
                dve.wait_ge(rows_ready, g * 4 + 4)
                link(nc.vector.reduce_sum(tiny[:, 13:14], sums[0][:, 0:SUM_COLS], mybir.AxisListType.X))
                nc.vector.tensor_scalar(minus_shift[:, phase:phase + 1], tiny[:, 13:14], -1.0 / PIX, None,
                                        ALU.mult).then_inc(shift_ready, 1)

            def step(g, p, b, phase, first=False, input_ready=None):
                lo_direct(g, p)
                take_group(g, p, b, 0)
                if input_ready is not None:
                    input_ready(0)
                    make_v(g + 1, p + 1, 0)
                    lo_group(g + 1, 0)
                take_group(g, p, b, 1)
                if input_ready is not None:
                    input_ready(1)
                    make_v(g + 1, p + 1, 1)
                    lo_group(g + 1, 1)
                if first:
                    find_shift(g, phase)
                else:
                    add_totals(g - 1, 1 - b, phase)

            def batchnorm_affine(phase):
                dve.wait_ge(totalled, IMAGES * (phase + 1))
                n = float(IMAGES * PIX)
                al = alpha[:, phase:phase + 1]
                gm, be = (gb[:, 2 * phase + k:2 * phase + k + 1] for k in range(2))
                total, squares_total, off, var = (tiny[:, k:k + 1] for k in (13, 14, 8, 9))
                v, r, t, minus_mean = tiny[:, 0:1], tiny[:, 1:2], tiny[:, 10:11], tiny[:, 12:13]
                link(nc.vector.reduce_sum(total, totals[:, phase, 0:SUM_COLS], mybir.AxisListType.X))
                link(nc.vector.tensor_scalar(off, total, 1.0 / n, minus_shift[:, phase:phase + 1], ALU.mult, ALU.add))
                link(nc.vector.tensor_scalar(t, off, off, None, ALU.mult))
                link(nc.vector.reduce_sum(squares_total, totals[:, phase, SUM_COLS:COLS], mybir.AxisListType.X))
                link(nc.vector.scalar_tensor_tensor(out=var, in0=squares_total, scalar=1.0 / n, in1=t,
                                                    op0=ALU.mult, op1=ALU.subtract))
                link(nc.vector.tensor_scalar(t, var, 0.0, alpha_squared[:, phase:phase + 1], ALU.max, ALU.mult))
                nc.vector.tensor_scalar(v, t, BN_EPS, None, ALU.add).then_inc(var_ready, 1)
                link(nc.vector.tensor_scalar(minus_mean, total, -1.0 / n, None, ALU.mult))
                dve.wait_ge(small_landed, 4 * 16)
                link(nc.vector.tensor_scalar(tiny[:, 11:12], al, gm, None, ALU.mult))
                dve.wait_ge(var_ready, phase + 1)
                dve.wait_ge(powed, phase + 1)
                link(nc.vector.tensor_scalar(t, r, r, v, ALU.mult, ALU.mult))
                link(nc.vector.tensor_scalar(var, t, -0.5, 1.5, ALU.mult, ALU.add))
                link(nc.vector.tensor_scalar(affine[:, phase, 0:1], var, r, tiny[:, 11:12], ALU.mult, ALU.mult))
                nc.vector.tensor_scalar(affine[:, phase, 1:2], minus_mean, affine[:, phase, 0:1], be,
                                        ALU.mult, ALU.add).then_inc(affine_ready, 1)

            def phase1(n, b, first=False):
                def x_ready(t):
                    if t == 0:
                        dve.wait_ge(x_landed[1 - b], (n + 1) // 2 * 16 + 16)
                step(n, n, b, 0, first, x_ready)

            dve.wait_ge(w_landed[0], 16)
            taps_to_integers(nc.vector, 0, link)
            dve.wait_ge(zeros_ready, 2)
            dve.wait_ge(x0_top_landed, 16)

            def sums_of_w1():
                dve.wait_ge(w_int_ready[0], 1)
                sum_taps(nc.vector, 0, link)

            first_group(0, 0, 0, sums_of_w1)
            dve.wait_ge(x_landed[0], 16)
            make_v(0, 0, 1)
            lo_group(0, 1)
            phase1(0, 0, first=True)
            phase1(1, 1)
            with dve.Fori(1, (IMAGES - 2) // 2) as i:
                for b in range(2):
                    phase1(i * 2 + b, b)
            phase1(IMAGES - 2, 0)
            step(IMAGES - 1, IMAGES - 1, 1, 0)
            add_totals(IMAGES - 1, 1, 0)
            batchnorm_affine(0)

            def phase2(m, b, first=False):
                def relu_over(t):
                    dve.wait_ge(relu_ready, m * 3 + (t + 4))
                step(m + IMAGES, m + SPILL, b, 1, first, relu_over)

            dve.wait_ge(relu_ready, 1)
            first_group(IMAGES, SPILL, 1)
            dve.wait_ge(relu_ready, 2)
            make_v(IMAGES, SPILL, 1)
            lo_group(IMAGES, 1)
            phase2(0, 0, first=True)
            phase2(1, 1)
            with dve.Fori(1, (IMAGES - 2) // 2) as i:
                for b in range(2):
                    phase2(i * 2 + b, b)
            phase2(IMAGES - 2, 0)
            step(STEPS - 1, SPILL + IMAGES - 1, 1, 1)
            add_totals(STEPS - 1, 1, 1)
            batchnorm_affine(1)
            dve.wait_ge(affine_ready, 2)

            def add_residual(q, i, b, spilled):
                dve.wait_ge(res_landed[b], i * 16 + 16)
                if spilled:
                    dve.wait_ge(y2_landed[b], (i - (-(-(SLOTS - b) // XBUFS) - 1)) * 16)
                z = slot(q + 2 * SPILL)
                nc.vector.scalar_tensor_tensor(out=z, in0=z, scalar=affine[:, 1, 0:1], in1=xbuf[b][:, :],
                                               op0=ALU.mult, op1=ALU.add).then_inc(added, 1)

            in_lots(dve, 0, add_residual)

        @block.tensor
        def _(pe):
            def transpose_weights(k):
                for h, (first, end) in enumerate(W_LOTS):
                    pe.wait_ge(w_int_ready[k], 1 if end <= TAPS else 2)
                    for t in range(first, end):
                        last = nc.tensor.transpose(w_bank(k, h)[:, (t - first) * C:(t - first + 1) * C],
                                                   w_int[k][:, t * C:(t + 1) * C], ident[:, :])
                    last.then_inc(transposed, 1)

            def v_of(plane, k, shift):
                if k < 2:
                    return window(plane, k * PAIRS, (k + 1) * PAIRS, shift)
                both = window(plane, 2 * PAIRS, 4 * PAIRS, shift)
                return both.rearrange("c (r two) w -> c r two w", two=2)[:, :, k - 2, :]

            def group(g, t, w, first_step, phase_starts):
                if not first_step:
                    pe.wait_ge(evac_done, g * NC + ((2 if t == 0 else 3) - NC))
                v1_alone = phase_starts is not None and t == 0
                for k in range(M_BANKS):
                    if v1_alone and k == 0:
                        pe.wait_ge(v1_lo_ready, phase_starts + 1)
                    if k in ((1, 2) if v1_alone else (0, 2)):
                        pe.wait_ge(lo_ready, g * SPLITS + (2 * t + k // 2 + 1))
                    for kw in range(3):
                        for half in range(2):
                            last = nc.tensor.matmul(rows_of(psum[:, GROUP_BANK[t] + k, 0:N]),
                                                    w[:, M_WEIGHT[k] + kw, :],
                                                    v_of(v_plane[t][half], k, kw - 1),
                                                    start=(kw == 0 and half == 0), stop=(kw == 2 and half == 1))
                    last.then_inc(m_done, 1)

            taps = sorted(((kh, kw) for kh in range(3) for kw in range(3)), key=lambda t: t != (1, 1))

            def chunk(g, j, w):
                if j == 0:
                    pe.wait_ge(lo_ready, g * SPLITS + SPLITS)
                pe.wait_ge(rows_ready, g * 4 + (2 if CHUNK_BANK[j] < 4 else 4))
                for n, (kh, kw) in enumerate(taps):
                    r0 = CHUNKS[j][0] + kh - 1
                    r1 = min(H, CHUNKS[j][1] + kh - 1)
                    for half in range(2):
                        last = nc.tensor.matmul(rows_of(psum[:, CHUNK_BANK[j], 0:(r1 - r0) * W]),
                                                w[:, kh * 3 + kw, :],
                                                window(d_plane[half], r0 - DIRECT0 + 1, r1 - DIRECT0 + 1, kw - 1),
                                                start=(n == 0 and half == 0), stop=(n == TAPS - 1 and half == 1))
                last.then_inc(chunk_done, 1)

            def convolve(g, w, first_step=False, phase_starts=None, w2_taken=False):
                for t in range(GROUPS):
                    if w2_taken and t == 1:
                        pe.wait_ge(wT_ready, 4)
                    group(g, t, w, first_step, phase_starts)
                for j in range(NC):
                    chunk(g, j, w)

            pe.wait_ge(ident_ready, 1)
            transpose_weights(0)
            pe.wait_ge(wT_ready, 2)
            pe.wait_ge(pads_ready, PADS)
            convolve(0, wT[0], first_step=True, phase_starts=0)
            convolve(1, wT[0])
            transpose_weights(1)
            convolve(2, wT[0], w2_taken=True)
            convolve(3, wT[0])
            with pe.Fori(2, IMAGES // 2) as i:
                for b in range(2):
                    convolve(i * 2 + b, wT[0])
            convolve(IMAGES, wT[1], phase_starts=1)
            convolve(IMAGES + 1, wT[1])
            with pe.Fori(IMAGES // 2 + 1, IMAGES) as i:
                for b in range(2):
                    convolve(i * 2 + b, wT[1])


_INS = ["x", "L0_conv_w1", "L0_conv_alpha1", "L0_conv_gamma1", "L0_conv_beta1",
        "L0_conv_w2", "L0_conv_alpha2", "L0_conv_gamma2", "L0_conv_beta2"]


def kernel(**inputs):
    import concourse.bacc as bacc
    from concourse.bass_utils import run_bass_kernel_spmd

    nc = bacc.Bacc("TRN2", target_bir_lowering=False, num_devices=1, dynamic_dma_scratch_size=1024)
    arrays, args = {}, []
    for name in _INS:
        a = np.ascontiguousarray(inputs[name])
        arrays[f"in_{name}"] = a
        args.append(nc.dram_tensor(f"in_{name}", a.shape, mybir.dt.from_np(a.dtype), kind="ExternalInput").ap())
    o = nc.dram_tensor("out", arrays["in_x"].shape, F32, kind="ExternalOutput").ap()
    residual_block(nc, *args, o)
    r = run_bass_kernel_spmd(nc, [arrays], core_ids=[0])
    return r.results[0]["out"]
```
